# Optimizing a Trainium2 kernel written in Bass

```python
import numpy as np
import jax
import jax.numpy as jnp

def _softmax(x, axis=-1):
    return jax.nn.softmax(x, axis=axis)

def _gelu(x):
    return jax.nn.gelu(x, approximate=True)

def _silu(x):
    return jax.nn.silu(x)

def _sigmoid(x):
    return jax.nn.sigmoid(x)

def _layernorm(x, axis=-1, eps=1e-05):
    m = jnp.mean(x, axis=axis, keepdims=True)
    v = jnp.var(x, axis=axis, keepdims=True)
    return (x - m) / jnp.sqrt(v + eps)

def _scatter_add(tgt, idx, src, axis=0):
    return tgt.at[idx].add(src)

def _segment_sum(src, seg, n):
    return jax.ops.segment_sum(src, seg, n)
kernel_name = 'mk_xattn_seq_d1_seqx_r4_61881b'

def setup_inputs(seed: int=0):
    np.random.seed(seed)
    _w = jnp.asarray

    def _rec_inputs():
        import jax
        import jax.numpy as jnp
        _rk = jax.random.key(seed)
        x = -0.000296 + 1 * jax.random.normal(jax.random.fold_in(_rk, 1), (8, 512, 320), jnp.float32)
        _lenS = 512 - jax.random.randint(jax.random.fold_in(_rk, 7), (8,), 0, max(1, 512 // 4) + 1, jnp.int32)
        _lenS2 = 1601 - jax.random.randint(jax.random.fold_in(_rk, 8), (8,), 0, max(1, 1601 // 4) + 1, jnp.int32)
        _ctx_2048P = jax.random.normal(jax.random.fold_in(_rk, 11), (8, 16, 512), jnp.float32)
        _ctx_2048c = jax.random.dirichlet(jax.random.fold_in(_rk, 511), 0.3 * jnp.ones((16,), jnp.float32), (8, 1601))
        _ctx_2048t = jnp.einsum('bsk,bkd->bsd', _ctx_2048c, _ctx_2048P)
        _ctx_2048t = _ctx_2048t * jax.lax.rsqrt(jnp.mean(jnp.square(_ctx_2048t)) + 1e-12) * 0.953939
        ctx_2048 = 0.00118529 + 0.99962 * (_ctx_2048t + 0.3 * jax.random.normal(jax.random.fold_in(_rk, 611), (8, 1601, 512), jnp.float32))
        fside_Bx4x4_0 = jax.random.uniform(jax.random.fold_in(_rk, 12), (8, 4, 4), jnp.float32, 0.0, 0.981965)
        return (x, ctx_2048, fside_Bx4x4_0)
    x, ctx_2048, fside_Bx4x4_0 = _rec_inputs()

    def _L0_xattn_setup():
        import jax, jax.numpy as jnp
        import numpy as np
        HEADS = 20
        NUM_IP_TOKENS = 4
        NUM_DUMMY_TOKENS = 4
        IP_SCALE = 1.0
        ASPECT_RATIO = 1.0
        NEG = -10000.0

        def _grid_hw(seq_len, aspect_ratio):
            width = int((seq_len / aspect_ratio) ** 0.5)
            height = seq_len // width
            while width * height != seq_len:
                if width * height < seq_len:
                    width += 1
                else:
                    width -= 1
                height = seq_len // width
            return (height, width)

        def _sdpa(q, k, v, mask=None):
            dh = q.shape[-1]
            scores = jnp.einsum('bhqd,bhkd->bhqk', q, k) / jnp.sqrt(jnp.asarray(dh, q.dtype))
            if mask is not None:
                scores = scores + mask
            probs = jax.nn.softmax(scores, axis=-1)
            return jnp.einsum('bhqk,bhkd->bhqd', probs, v)

        def _split_heads(x, heads):
            b, l, d = x.shape
            return x.reshape(b, l, heads, d // heads).transpose(0, 2, 1, 3)

        def _merge_heads(x):
            b, h, l, dh = x.shape
            return x.transpose(0, 2, 1, 3).reshape(b, l, h * dh)

        def _ip_mask(bbox, batch_size, seq_len, dtype):
            M = bbox.shape[1]
            height, width = _grid_hw(seq_len, ASPECT_RATIO)
            x = jnp.linspace(0.0, 1.0, width, dtype=dtype)
            y = jnp.linspace(0.0, 1.0, height, dtype=dtype)
            yg, xg = jnp.meshgrid(y, x, indexing='ij')
            xg = xg.reshape(-1)
            yg = yg.reshape(-1)
            x1, y1, x2, y2 = (bbox[..., 0:1], bbox[..., 1:2], bbox[..., 2:3], bbox[..., 3:4])
            inside = (xg >= x1) & (xg <= x2) & (yg >= y1) & (yg <= y2)
            ip_mask = jnp.where(inside, 0.0, NEG).astype(dtype)
            ip_mask = jnp.transpose(ip_mask, (0, 2, 1))[:, None]
            ip_mask = jnp.repeat(ip_mask, NUM_IP_TOKENS // M, axis=-1)
            dummy = jnp.where(jnp.any(inside, axis=1), NEG, 0.0).astype(dtype)
            dummy = jnp.repeat(dummy[:, None, :, None], NUM_DUMMY_TOKENS, axis=-1)
            return jnp.concatenate([dummy, ip_mask], axis=-1)
        key = jax.random.key(seed)
        ks = jax.random.split(key, 12)
        B, S, D, C = (4, 1024, 320, 512)
        text_len, M = (77, 4)
        hidden_states = jax.random.normal(ks[0], (B, S, D), jnp.float32)
        encoder_hidden_states = jax.random.normal(ks[1], (B, text_len + NUM_IP_TOKENS + NUM_DUMMY_TOKENS, C), jnp.float32)
        p1 = jax.random.uniform(ks[2], (B, M, 2), jnp.float32)
        p2 = jax.random.uniform(ks[3], (B, M, 2), jnp.float32)
        bbox = jnp.concatenate([jnp.minimum(p1, p2), jnp.maximum(p1, p2)], axis=-1)
        s = 0.02
        w_q = jax.random.normal(ks[4], (D, D), jnp.float32) * s
        w_k = jax.random.normal(ks[5], (C, D), jnp.float32) * s
        w_v = jax.random.normal(ks[6], (C, D), jnp.float32) * s
        w_k_ip = jax.random.normal(ks[7], (C, D), jnp.float32) * s
        w_v_ip = jax.random.normal(ks[8], (C, D), jnp.float32) * s
        w_out = jax.random.normal(ks[9], (D, D), jnp.float32) * s
        b_out = jnp.zeros((D,), jnp.float32)
        return {'hidden_states': hidden_states, 'encoder_hidden_states': encoder_hidden_states, 'bbox': bbox, 'w_q': w_q, 'w_k': w_k, 'w_v': w_v, 'w_k_ip': w_k_ip, 'w_v_ip': w_v_ip, 'w_out': w_out, 'b_out': b_out}
    _L0_xattn_all = _L0_xattn_setup()
    _L0_xattn_in = {k: v for k, v in _L0_xattn_all.items() if k in ('w_q', 'w_k', 'w_v', 'w_k_ip', 'w_v_ip', 'w_out', 'b_out')}
    del _L0_xattn_all
    return {'x': x, 'ctx_2048': ctx_2048, 'fside_Bx4x4_0': fside_Bx4x4_0, 'L0_xattn_w_q': _L0_xattn_in['w_q'], 'L0_xattn_w_k': _L0_xattn_in['w_k'], 'L0_xattn_w_v': _L0_xattn_in['w_v'], 'L0_xattn_w_k_ip': _L0_xattn_in['w_k_ip'], 'L0_xattn_w_v_ip': _L0_xattn_in['w_v_ip'], 'L0_xattn_w_out': _L0_xattn_in['w_out'], 'L0_xattn_b_out': _L0_xattn_in['b_out']}

def reference(x, ctx_2048, fside_Bx4x4_0, L0_xattn_w_q, L0_xattn_w_k, L0_xattn_w_v, L0_xattn_w_k_ip, L0_xattn_w_v_ip, L0_xattn_w_out, L0_xattn_b_out):
    import jax
    import jax.numpy as jnp

    def _L0_xattn_ref(hidden_states, encoder_hidden_states, bbox, w_q, w_k, w_v, w_k_ip, w_v_ip, w_out, b_out):
        import jax, jax.numpy as jnp
        import numpy as np
        HEADS = 20
        NUM_IP_TOKENS = 4
        NUM_DUMMY_TOKENS = 4
        IP_SCALE = 1.0
        ASPECT_RATIO = 1.0
        NEG = -10000.0

        def _grid_hw(seq_len, aspect_ratio):
            width = int((seq_len / aspect_ratio) ** 0.5)
            height = seq_len // width
            while width * height != seq_len:
                if width * height < seq_len:
                    width += 1
                else:
                    width -= 1
                height = seq_len // width
            return (height, width)

        def _sdpa(q, k, v, mask=None):
            dh = q.shape[-1]
            scores = jnp.einsum('bhqd,bhkd->bhqk', q, k) / jnp.sqrt(jnp.asarray(dh, q.dtype))
            if mask is not None:
                scores = scores + mask
            probs = jax.nn.softmax(scores, axis=-1)
            return jnp.einsum('bhqk,bhkd->bhqd', probs, v)

        def _split_heads(x, heads):
            b, l, d = x.shape
            return x.reshape(b, l, heads, d // heads).transpose(0, 2, 1, 3)

        def _merge_heads(x):
            b, h, l, dh = x.shape
            return x.transpose(0, 2, 1, 3).reshape(b, l, h * dh)

        def _ip_mask(bbox, batch_size, seq_len, dtype):
            M = bbox.shape[1]
            height, width = _grid_hw(seq_len, ASPECT_RATIO)
            x = jnp.linspace(0.0, 1.0, width, dtype=dtype)
            y = jnp.linspace(0.0, 1.0, height, dtype=dtype)
            yg, xg = jnp.meshgrid(y, x, indexing='ij')
            xg = xg.reshape(-1)
            yg = yg.reshape(-1)
            x1, y1, x2, y2 = (bbox[..., 0:1], bbox[..., 1:2], bbox[..., 2:3], bbox[..., 3:4])
            inside = (xg >= x1) & (xg <= x2) & (yg >= y1) & (yg <= y2)
            ip_mask = jnp.where(inside, 0.0, NEG).astype(dtype)
            ip_mask = jnp.transpose(ip_mask, (0, 2, 1))[:, None]
            ip_mask = jnp.repeat(ip_mask, NUM_IP_TOKENS // M, axis=-1)
            dummy = jnp.where(jnp.any(inside, axis=1), NEG, 0.0).astype(dtype)
            dummy = jnp.repeat(dummy[:, None, :, None], NUM_DUMMY_TOKENS, axis=-1)
            return jnp.concatenate([dummy, ip_mask], axis=-1)
        B, S, D = hidden_states.shape
        residual = hidden_states
        end_pos = encoder_hidden_states.shape[1] - (NUM_IP_TOKENS + NUM_DUMMY_TOKENS)
        text = encoder_hidden_states[:, :end_pos]
        ip_h = encoder_hidden_states[:, end_pos:]
        q = _split_heads(hidden_states @ w_q, HEADS)
        k = _split_heads(text @ w_k, HEADS)
        v = _split_heads(text @ w_v, HEADS)
        out_text = _sdpa(q, k, v)
        out_text = _merge_heads(out_text)
        mask_ip = _ip_mask(bbox, B, S, hidden_states.dtype)
        k_ip = _split_heads(ip_h @ w_k_ip, HEADS)
        v_ip = _split_heads(ip_h @ w_v_ip, HEADS)
        out_ip = _merge_heads(_sdpa(q, k_ip, v_ip, mask=mask_ip))
        out = out_text + IP_SCALE * out_ip
        out = out @ w_out + b_out
        out = out + residual
        return out
    x = _L0_xattn_ref(x, ctx_2048, fside_Bx4x4_0, L0_xattn_w_q, L0_xattn_w_k, L0_xattn_w_v, L0_xattn_w_k_ip, L0_xattn_w_v_ip, L0_xattn_w_out, L0_xattn_b_out)
    return x

_drawn_inputs = setup_inputs


def setup_inputs(seed=0):
    import zlib

    import numpy as np

    out = dict(_drawn_inputs(seed))
    spreads = {'L0_xattn_b_out': (0.0, 0.1)}
    factors = {'L0_xattn_w_q': 5.496, 'L0_xattn_w_k': 8.0, 'L0_xattn_w_k_ip': 6.088}
    for name, (base, spread) in spreads.items():
        noise = np.random.default_rng([zlib.crc32(name.encode()), seed]).standard_normal(out[name].shape)
        drawn = base * np.exp(spread * noise) if base else spread * noise
        out[name] = jnp.asarray(drawn.astype(out[name].dtype))
    for name, factor in factors.items():
        out[name] = (out[name] * factor).astype(out[name].dtype)
    return out
```

```python
import numpy as np
import concourse.bass as bass
from concourse import mybir
from contextlib import ExitStack

FP32 = mybir.dt.float32
BF16 = mybir.dt.bfloat16
ALU = mybir.AluOpType
ACT = mybir.ActivationFunctionType
AX = mybir.AxisListType

B, S, D, C = 8, 512, 320, 512
HEADS, DH = 20, 16
TOKENS = 1601
IPT = 8
TEXT = TOKENS - IPT
KEYS = 1600
GH = 4
NG = HEADS // GH
GR = GH * DH
CT = C // 128
QT = S // 128
FULL = KEYS // 128
TAIL = KEYS - FULL * 128
TAILV = TEXT - FULL * 128
KT = FULL + 1
HALF = KEYS // 2
CHUNK = HALF // 2
QHALF = S // 2
VW = DH + 1
PARTS = 3
K_BLOCKS = (0, 0, 0, 1, 1, 2)
Q_BLOCKS = (0, 1, 2, 0, 1, 0)
STACK = len(K_BLOCKS) * DH
ROWS = STACK + PARTS
SLOTS = (0, 1, 2, 3, 2)
EXPS = FULL * GH + GH // 2
UNITS = GH * QT * 2
SCALE = float(DH) ** -0.5
NEG = -10000.0
GRID_W, GRID_H = 32, 16


def work_plan(first, last):
    plan = {(0, 0): ("V", FULL - 1), (0, 1): ("V", FULL), (0, 6): ("Q", 2), (0, 7): ("IP", 2),
            (1, 7): ("Q", 3), (1, 9): ("IP", 3),
            (2, 7): ("WA",), (2, 9): ("WB",), (2, 11): ("Q", 4), (2, 12): ("IP", 4),
            (4, 0): ("TA",), (4, 1): ("TB",)}
    k_turns = {2: ((0, 2), (0, 3), (0, 4), (0, 5)), 3: ((1, 0), (1, 2), (1, 4), (1, 6)),
               4: ((1, 11), (1, 12), (2, 1), (2, 3))}
    if not first:
        plan.update({(0, 9 + t): ("OUT", t) for t in range(QT)})
    if not last:
        k_turns.update({5: ((3, 0), (3, 1), (3, 2), (3, 3)), 6: ((3, 6), (3, 7), (3, 8), (3, 9))})
        plan.update({(3, 4): ("Q", 5), (3, 5): ("IP", 5), (3, 11): ("Q", 6), (3, 12): ("IP", 6)})
        plan.update({(4, 2 + t): ("V", t) for t in range(FULL - 1)})
    for group, turns in k_turns.items():
        plan.update({at: ("K", group, n // 2, n % 2) for n, at in enumerate(turns)})
    return plan


SPLITS = ((("K", 2, 0), ("K", 2, 1), ("Q", 2)), (("K", 3, 0), ("K", 3, 1), ("Q", 3), ("K", 4, 0)), (("K", 4, 1), ("Q", 4)),
          (("K", 5, 0), ("K", 5, 1), ("Q", 5), ("K", 6, 0), ("K", 6, 1), ("Q", 6)), ())
NEG_AT = 11


def work_order(first, last):
    plan, order = work_plan(first, last), {}
    for g in range(NG):
        for kt in range(KT):
            if kt == NEG_AT and not (last and g == NG - 1):
                order["NEG", g + 1] = len(order)
            piece = plan.get((g, kt))
            if piece is not None and (piece[0] != "K" or piece[3] == 0):
                order[piece[:3] if piece[0] == "K" else piece] = len(order)
    return order


PRO = [("KIP",), ("VIP",)] + [p for g in (0, 1) for p in (("K", g, 0), ("K", g, 1), ("Q", g), ("IP", g))]
PRO += [("V", t) for t in range(FULL - 1)] + [("NEG", 0)]
PRO_ORDER = {p: n for n, p in enumerate(PRO)}
FIRST_WORK = len(work_order(True, False))
LOOP_WORK = len(work_order(False, False))


UNITS_AT = ((3, 3, 4, 4, 3, 3, 3, 2, 2, 3, 2), (4, 2, 4, 2, 4, 2, 4, 3, 2, 3, 2), (3, 4, 3, 4, 3, 3, 2, 3, 3, 3, 1),
            (0, 0, 0, 4, 4, 4, 5, 4, 4, 4, 3), (2, 3, 4, 3, 3, 3, 3, 3, 3, 3, 2))
PLACES = ((0, 0, 0, 0), (1, 0, 0, 0), (0, 0, 2, 0), (1, 0, 1, 1), (1, 1, 1, 1), (2, 1, 1, 1))
LAST_PLACES = ((0, 0, 0, 0), (1, 0, 0, 0), (1, 1, 0, 0), (1, 1, 1, 0))
assert all(sum(u) == UNITS for u in UNITS_AT)


def units_at(g, kt):
    if kt >= len(UNITS_AT[g]):
        return PLACES[0]
    return (LAST_PLACES if kt == len(UNITS_AT[g]) - 1 else PLACES)[UNITS_AT[g][kt]]


def exps_of(kt):
    return range(GH) if kt < FULL else range(GH // 2)


def cross_attention(nc, x, x_t, ctx_t, ctx_ip_t, boxes, grid, own_rows, ident, w_q, w_k, w_v, w_k_ip, w_v_ip,
                    w_out, b_out, out):
    scratch_k = nc.dram_tensor("scratch_k", (NG, PARTS, GR, KEYS), BF16, kind="Internal").ap()
    scratch_q = nc.dram_tensor("scratch_q", (NG, PARTS, GR, S), BF16, kind="Internal").ap()
    scratch_r = nc.dram_tensor("scratch_r", (GH, S), FP32, kind="Internal").ap()

    ctx = ExitStack()
    with ctx:
        def sb(name, shape, dt=FP32):
            return ctx.enter_context(nc.sbuf_tensor(name, shape, dt))

        def sem(name):
            return ctx.enter_context(nc.semaphore(name))

        wq = sb("wq", [128, 3, D])
        wk = sb("wk", [128, CT, D])
        wv = sb("wv", [128, CT, D])
        wout = sb("wout", [128, 4, D])
        own = sb("own", [128, 8])
        ident_f = sb("ident_f", [128, 128])
        ident_b = sb("ident_b", [128, 128], BF16)
        grid_sb = sb("grid_sb", [128, 2, QT])
        box = sb("box", [128, B, 4, 4])
        inside = sb("inside", [128, B, QT, 4])
        cmp = sb("cmp", [128, B, QT, 4])
        outside = sb("outside", [128, B, QT])
        mask = sb("mask", [128, B, QT, IPT])
        ctxt = sb("ctxt", [128, CT, KEYS])
        xt = sb("xt", [128, 3, S])
        xres = sb("xres", [128, QT, D])
        k_parts = sb("k_parts", [128, PARTS, HALF], BF16)
        k_rest = sb("k_rest", [128, 2, CHUNK])
        q_full = sb("q_full", [128, QHALF])
        q_rest = sb("q_rest", [128, QHALF])
        q_parts = sb("q_parts", [128, PARTS, QHALF], BF16)
        k_stack = sb("k_stack", [128, 4, GH, KEYS], BF16)
        q_stack = sb("q_stack", [128, 4, GH, S], BF16)
        v_ones = sb("v_ones", [128, KT, HEADS * VW])
        probs = sb("probs", [128, 2, GH, S])
        probs_tail = sb("probs_tail", [128, GH // 2, S])
        half_max = sb("half_max", [128, UNITS])
        neg_max = sb("neg_max", [128, UNITS // 2])
        neg_rest = sb("neg_rest", [128, UNITS // 2])
        neg_parts = sb("neg_parts", [128, 8, UNITS // 2], BF16)
        neg_rows = sb("neg_rows", [PARTS * UNITS // 2, 128], BF16)
        zero = sb("zero", [128, 1])
        o_sum = sb("o_sum", [128, S])
        sums = sb("sums", [128, GH * S // 128])
        recips = sb("recips", [128, GH * S // 128])
        r_wide = sb("r_wide", [128, S])
        o_t = sb("o_t", [128, 4, S])
        out_sb = sb("out_sb", [128, 2, D])
        kip = sb("kip", [128, NG, B * IPT])
        vip = sb("vip", [128, 3, B * IPT])
        kip_own = sb("kip_own", [128, NG, 8, IPT])
        vip_own = sb("vip_own", [128, 3, 8, IPT])
        s_ip = sb("s_ip", [128, QT, HEADS * IPT])
        p_ip = sb("p_ip", [128, QT, HEADS * IPT])
        ip_max = sb("ip_max", [128, QT, HEADS])
        ip_sum = sb("ip_sum", [128, QT, HEADS])
        early = probs[:, :, :, :].rearrange("p a h n -> p (a h n)")
        wk_ip = early[:, 0:CT * D].rearrange("p (c n) -> p c n", c=CT)
        wv_ip = early[:, CT * D:2 * CT * D].rearrange("p (c n) -> p c n", c=CT)
        ctx_ip = early[:, 2 * CT * D:2 * CT * D + CT * B * IPT].rearrange("p (c n) -> p c n", c=CT)

        exp_bank = ctx.enter_context(nc.psum_tensor("exp_bank", [128, 2, 512], FP32))
        max_bank = ctx.enter_context(nc.psum_tensor("max_bank", [128, 4, 512], FP32))
        pv_bank = ctx.enter_context(nc.psum_tensor("pv_bank", [128, 512], FP32))
        work_bank = ctx.enter_context(nc.psum_tensor("work_bank", [128, 512], FP32))

        weights_ip_loaded = sem("weights_ip_loaded")
        weights_loaded = sem("weights_loaded")
        consts_loaded = sem("consts_loaded")
        ctx_loaded = sem("ctx_loaded")
        x_loaded = sem("x_loaded")
        residual_loaded = sem("residual_loaded")
        cleared = sem("cleared")
        mask_step = sem("mask_step")
        k_high = sem("k_high")
        k_mid = sem("k_mid")
        k_split = sem("k_split")
        k_stored = sem("k_stored")
        q_step = sem("q_step")
        q_stored = sem("q_stored")
        stack_loaded = [sem(f"stack_loaded{g}") for g in range(NG)]
        scores_ready = sem("scores_ready")
        probs_ready = sem("probs_ready")
        pv_done = sem("pv_done")
        max_scores = sem("max_scores")
        max_taken = sem("max_taken")
        neg_step = sem("neg_step")
        neg_loaded = sem("neg_loaded")
        o_read = sem("o_read")
        sums_loaded = sem("sums_loaded")
        recips_ready = sem("recips_ready")
        recips_stored = sem("recips_stored")
        r_wide_loaded = sem("r_wide_loaded")
        o_scaled = sem("o_scaled")
        o_packed = sem("o_packed")
        kip_ready = sem("kip_ready")
        vip_ready = sem("vip_ready")
        ip_step = sem("ip_step")
        ip_exp = sem("ip_exp")
        ip_exp_sum = sem("ip_exp_sum")
        ones_ready = sem("ones_ready")
        work_full = sem("work_full")
        work_empty = sem("work_empty")
        out_stored = [sem(f"out_stored{i}") for i in range(2)]

        def work_number(b, piece, first, last):
            local = work_order(first, last)[piece]
            if first:
                return len(PRO) + local
            return b * LOOP_WORK + (len(PRO) + FIRST_WORK - LOOP_WORK + local)

        def batches(eng, body):
            body(0, True, False)
            with eng.Fori(1, B - 1) as b:
                body(b, False, False)
            body(B - 1, False, True)

        block = ctx.enter_context(nc.Block())

        @block.sync
        def _(sp):
            def store_k(b, g):
                sp.wait_ge(k_split, (b * NG + g) * 2 + 2)
                for half in range(2):
                    sp.dma_start(scratch_k[g % NG, :, :, half * HALF:(half + 1) * HALF].rearrange("a r n -> r a n"),
                                 k_parts[half * GR:(half + 1) * GR, :, :]).then_inc(k_stored, 16)

            def store_q(b, g):
                sp.wait_ge(q_step, (b * NG + g) * 4 + 4)
                for half in range(2):
                    sp.dma_start(scratch_q[g % NG, :, :, half * QHALF:(half + 1) * QHALF].rearrange("a r n -> r a n"),
                                 q_parts[half * GR:(half + 1) * GR, :, :]).then_inc(q_stored, 16)

            def slot_free(b, g, early_batch):
                if g == 4:
                    sp.wait_ge(scores_ready, (b * NG + g - 1) * EXPS)
                elif g == 2:
                    if not early_batch:
                        sp.wait_ge(scores_ready, (b * NG + g - 2) * EXPS)
                elif not early_batch:
                    sp.wait_ge(scores_ready, (b * NG + g - NG + 1) * EXPS)

            def load_k(b, g):
                sp.wait_ge(k_stored, (b * NG + g + 1) * 32)
                for n, part in enumerate(K_BLOCKS):
                    sp.dma_start(k_stack[n * DH:(n + 1) * DH, SLOTS[g % NG], :, :],
                                 scratch_k[g % NG, part].rearrange("(h i) n -> i h n", i=DH))\
                      .then_inc(stack_loaded[g % NG], 16)

            def load_q(b, g):
                sp.wait_ge(q_stored, (b * NG + g + 1) * 32)
                for n, part in enumerate(Q_BLOCKS):
                    sp.dma_start(q_stack[n * DH:(n + 1) * DH, SLOTS[g % NG], :, :],
                                 scratch_q[g % NG, part].rearrange("(h i) n -> i h n", i=DH))\
                      .then_inc(stack_loaded[g % NG], 16)

            def stack_group(b, g, early_batch):
                store_k(b, g)
                slot_free(b, g, early_batch)
                load_k(b, g)
                store_q(b, g)
                load_q(b, g)

            def load_ctx(b):
                for c in range(CT):
                    sp.dma_start(ctxt[:, c, :], ctx_t[b, c * 128:(c + 1) * 128, :]).then_inc(ctx_loaded, 16)

            def load_x(b):
                sp.dma_start(xt[:, 0:2, :], x_t[b, 0:256, :].rearrange("(c p) n -> p c n", p=128)).then_inc(x_loaded, 16)
                sp.dma_start(xt[0:64, 2, :], x_t[b, 256:D, :]).then_inc(x_loaded, 16)

            def normalise(group_no, g, out_done):
                sp.wait_ge(o_read, group_no + 1)
                sp.dma_start(sums[:, :], o_sum[DH:128:32, :]).then_inc(sums_loaded, 16)
                sp.wait_ge(recips_ready, group_no + 1)
                sp.dma_start(scratch_r.rearrange("h (c n) -> (h c) n", n=GH * S // 128), recips[:, :])\
                  .then_inc(recips_stored, 16)
                sp.wait_ge(recips_stored, (group_no + 1) * 16)
                sp.dma_start(r_wide[:, :], scratch_r.unsqueeze(1).to_broadcast([GH, 32, S])).then_inc(r_wide_loaded, 16)
                sp.wait_ge(o_scaled, group_no + 1)
                if out_done is not None:
                    sp.wait_ge(work_full, out_done + 1)
                for h in range(GH):
                    row = (g % 2) * GR + h * DH
                    sp.dma_start(o_t[row:row + DH, g // 2, :], o_sum[h * 32:h * 32 + DH, :]).then_inc(o_packed, 16)

            def store_out(b, t, number):
                sp.wait_ge(work_empty, number + 1)
                sp.dma_start(out[b, t * 128:(t + 1) * 128, :], out_sb[:, t % 2, :]).then_inc(out_stored[t % 2], 16)

            sp.dma_start(ctx_ip, ctx_ip_t.rearrange("(c p) n -> p c n", p=128)).then_inc(weights_ip_loaded, 16)
            sp.dma_start(wk_ip, w_k_ip.rearrange("(c p) n -> p c n", p=128)).then_inc(weights_ip_loaded, 16)
            sp.dma_start(wv_ip, w_v_ip.rearrange("(c p) n -> p c n", p=128)).then_inc(weights_ip_loaded, 16)
            sp.dma_start(wk[:, :, :], w_k.rearrange("(c p) n -> p c n", p=128)).then_inc(weights_loaded, 16)
            load_ctx(0)
            load_x(0)
            sp.dma_start(wq[:, 0:2, :], w_q[0:256, :].rearrange("(c p) n -> p c n", p=128)).then_inc(weights_loaded, 16)
            sp.dma_start(wq[0:64, 2, :], w_q[256:D, :]).then_inc(weights_loaded, 16)
            sp.dma_start(wv[:, :, :], w_v.rearrange("(c p) n -> p c n", p=128)).then_inc(weights_loaded, 16)
            sp.dma_start(wout[:, 0:2, :], w_out[0:256, :].rearrange("(c p) n -> p c n", p=128)).then_inc(weights_loaded, 16)
            sp.dma_start(wout[0:64, 2, :], w_out[256:D, :]).then_inc(weights_loaded, 16)
            sp.dma_start(wout[96:97, 2, :], b_out.unsqueeze(0)).then_inc(weights_loaded, 16)
            stack_group(0, 0, True)
            stack_group(0, 1, True)

            def body(b, first, last):
                number = lambda piece: work_number(b, piece, first, last)
                for g in range(NG):
                    group_no = b * NG + g
                    if g == 0 and not first:
                        sp.dma_start(xres[:, :, :], x[b - 1].rearrange("(t p) d -> p t d", p=128))\
                          .then_inc(residual_loaded, 16)
                    if g == 3:
                        slot_free(b, 4, first)
                        load_k(b, 4)
                        load_q(b, 4)
                    if g or not first:
                        normalise(group_no - 1, (g - 1) % NG, number(("OUT", QT - 1)) if g == 1 and not first else None)
                    if g < 2:
                        stack_group(b, g + 2, first)
                    elif g == 2:
                        store_k(b, 4)
                        if not last:
                            sp.wait_ge(work_full, number(("K", 4, 1)) + 1)
                            load_ctx(b + 1)
                        store_q(b, 4)
                        if not last:
                            sp.wait_ge(work_full, number(("Q", 4)) + 1)
                            load_x(b + 1)
                    elif g == 3:
                        if not last:
                            stack_group(b, 5, False)
                            stack_group(b, 6, False)
                    if g == 0 and not first:
                        for t in range(QT):
                            store_out(b - 1, t, number(("OUT", t)))

            batches(sp, body)
            end = len(PRO) + FIRST_WORK + (B - 2) * LOOP_WORK + len(work_order(False, True))
            sp.dma_start(xres[:, :, :], x[B - 1].rearrange("(t p) d -> p t d", p=128)).then_inc(residual_loaded, 16)
            normalise(B * NG - 1, NG - 1, None)
            for t in range(QT):
                store_out(B - 1, t, end + t)
            for i in range(2):
                sp.wait_ge(out_stored[i], B * QT // 2 * 16)

        @block.tensor
        def _(pe):
            def bank_free(number):
                if number is not None:
                    pe.wait_ge(work_empty, number)

            def k_piece(g, c, ct_range, number):
                for ct in ct_range:
                    for half in range(2):
                        keys = half * HALF + c * CHUNK
                        last = nc.tensor.matmul(work_bank[half * GR:(half + 1) * GR, 0:CHUNK],
                                                wk[:, ct, (g % NG) * GR:(g % NG + 1) * GR], ctxt[:, ct, keys:keys + CHUNK],
                                                start=(ct == 0), stop=(ct == CT - 1))
                if ct_range[-1] == CT - 1:
                    last.then_inc(work_full, 1)

            def q_piece(g, number):
                for ct, rows in enumerate((128, 128, 64)):
                    for half in range(2):
                        last = nc.tensor.matmul(work_bank[half * GR:(half + 1) * GR, 0:QHALF],
                                                wq[0:rows, ct, (g % NG) * GR:(g % NG + 1) * GR],
                                                xt[0:rows, ct, half * QHALF:(half + 1) * QHALF],
                                                start=(ct == 0), stop=(ct == 2))
                last.then_inc(work_full, 1)

            def ip_piece(g, q_number, kip_count):
                pe.wait_ge(work_empty, q_number + 1)
                pe.wait_ge(kip_ready, kip_count)
                for n in range(2):
                    last = nc.tensor.matmul(work_bank[:, n * 64:(n + 1) * 64], q_full[:, n * 128:(n + 1) * 128],
                                            kip_own[:, g % NG, :, :].rearrange("p h t -> p (h t)"), start=True, stop=True)
                last.then_inc(work_full, 1)

            def v_piece(t):
                if t < FULL:
                    for ct in range(CT):
                        last = nc.tensor.matmul(work_bank[:, 0:D], ctxt[:, ct, t * 128:(t + 1) * 128], wv[:, ct, :],
                                                start=(ct == 0), stop=(ct == CT - 1))
                else:
                    for ct in range(CT):
                        for odd in range(2):
                            last = nc.tensor.matmul(work_bank[odd * TAIL:odd * TAIL + TAILV, 0:D],
                                                    ctxt[:, ct, FULL * 128:TEXT], wv[:, ct, :],
                                                    start=(ct == 0), stop=(ct == CT - 1))
                last.then_inc(work_full, 1)

            def out_piece(t):
                for k, rows in enumerate((128, 128, 97, 128)):
                    last = nc.tensor.matmul(work_bank[:, 0:D], o_t[0:rows, k, t * 128:(t + 1) * 128], wout[0:rows, k, :],
                                            start=(k == 0), stop=(k == 3))
                last.then_inc(work_full, 1)

            def negative_piece(group_no):
                pe.wait_ge(neg_step, group_no * 5 + 5)
                nc.tensor.transpose(work_bank[:, :].bitcast(BF16)[:, 0:128],
                                    neg_parts[:, :, :].rearrange("p a m -> p (a m)"), ident_b[:, :]).then_inc(work_full, 1)

            def work(b, piece, first, last, kt, g):
                number = lambda p: work_number(b, p, first, last)
                kind = piece[0]
                if kind == "K":
                    if piece[3] == 0:
                        pe.wait_ge(work_empty, number(piece[:3]))
                        if piece[1] == 5 and piece[2] == 0:
                            pe.wait_ge(ctx_loaded, (b + 2) * CT * 16)
                    k_piece(piece[1], piece[2], range(2) if piece[3] == 0 else range(2, CT), None)
                    return
                pe.wait_ge(work_empty, number(piece))
                if kind == "Q":
                    if piece[1] == 5:
                        pe.wait_ge(x_loaded, (b + 2) * 32)
                    q_piece(piece[1], None)
                elif kind == "IP":
                    ip_piece(piece[1], number(("Q", piece[1])), b + (2 if piece[1] >= NG else 1))
                elif kind == "V":
                    v_piece(piece[1])
                elif kind == "OUT":
                    if piece[1] == 0:
                        pe.wait_ge(o_packed, b * NG * 64)
                    out_piece(piece[1])
                elif kind == "WA":
                    pe.wait_ge(vip_ready, b + 1)
                    nc.tensor.matmul(work_bank[64:128, 0:D], vip_own[:, 1, :, :].rearrange("p h t -> p (h t)"),
                                     wout[:, 1, :], start=True, stop=True).then_inc(work_full, 1)
                elif kind == "WB":
                    nc.tensor.matmul(work_bank[0:64, 0:D], vip_own[:, 0, :, :].rearrange("p h t -> p (h t)"),
                                     wout[:, 0, :], start=True, stop=True)
                    nc.tensor.matmul(work_bank[64:96, 0:D], vip_own[0:64, 2, 0:GH, :].rearrange("p h t -> p (h t)"),
                                     wout[0:64, 2, :], start=True, stop=True).then_inc(work_full, 1)
                elif kind == "TA":
                    pe.wait_ge(ip_step, b * 5 + 5)
                    for t in range(QT):
                        last_mm = nc.tensor.transpose(work_bank[:, t * 128:(t + 1) * 128], p_ip[:, t, 0:128], ident_f[:, :])
                    last_mm.then_inc(work_full, 1)
                elif kind == "TB":
                    for t in range(QT):
                        last_mm = nc.tensor.transpose(work_bank[0:96, t * 128:(t + 1) * 128], p_ip[:, t, 64:160], ident_f[:, :])
                    last_mm.then_inc(work_full, 1)

            def max_unit(group_no, g, u, first_group):
                h, t, half = u // (2 * QT), u // 2 % QT, u % 2
                if not (first_group and u < 2):
                    pe.wait_ge(max_taken, group_no * UNITS + u - 1)
                slot = SLOTS[g % NG]
                for c in range(2):
                    keys = half * HALF + c * CHUNK
                    last = nc.tensor.matmul(max_bank[:, (u % 2) * 2 + c, 0:CHUNK],
                                            q_stack[0:STACK, slot, h, t * 128:(t + 1) * 128],
                                            k_stack[0:STACK, slot, h, keys:keys + CHUNK], start=True, stop=True)
                last.then_inc(max_scores, 1)

            def exp_tile(group_no, g, kt, j, first_group):
                n, slot = kt * GH + j, SLOTS[g]
                if not (first_group and n < 2):
                    pe.wait_ge(probs_ready, group_no * EXPS + n - 1)
                if kt < FULL:
                    last = nc.tensor.matmul(exp_bank[:, n % 2, :], k_stack[0:ROWS, slot, j, kt * 128:(kt + 1) * 128],
                                            q_stack[0:ROWS, slot, j, :], start=True, stop=True)
                else:
                    for odd in range(2):
                        h = 2 * j + odd
                        last = nc.tensor.matmul(exp_bank[odd * TAIL:(odd + 1) * TAIL, n % 2, :],
                                                k_stack[0:ROWS, slot, h, FULL * 128:KEYS], q_stack[0:ROWS, slot, h, :],
                                                start=True, stop=True)
                last.then_inc(scores_ready, 1)

            def pv_tile(group_no, g, kt):
                pe.wait_ge(probs_ready, group_no * EXPS + kt * GH + len(exps_of(kt)))
                if kt == 0:
                    pe.wait_ge(o_read, group_no)
                for h in range(GH):
                    head = g * GH + h
                    p = probs[:, kt % 2, h, :] if kt < FULL else probs_tail[:, h // 2, :]
                    last = nc.tensor.matmul(pv_bank[h * 32:h * 32 + VW, :], v_ones[:, kt, head * VW:(head + 1) * VW], p,
                                            start=(kt == 0), stop=(kt == FULL))
                last.then_inc(pv_done, 1)

            pe.wait_ge(weights_ip_loaded, 48)
            for g in range(NG):
                for half in range(2):
                    for ct in range(CT):
                        last = nc.tensor.matmul(work_bank[half * GR:(half + 1) * GR, g * 64:(g + 1) * 64],
                                                wk_ip[:, ct, g * GR:(g + 1) * GR], ctx_ip[:, ct, :],
                                                start=(ct == 0), stop=(ct == CT - 1))
            last.then_inc(work_full, 1)
            pe.wait_ge(work_empty, 1)
            for m, rows in enumerate((128, 128, 64)):
                for ct in range(CT):
                    last = nc.tensor.matmul(work_bank[0:rows, m * 64:(m + 1) * 64],
                                            wv_ip[:, ct, m * 128:m * 128 + rows], ctx_ip[:, ct, :],
                                            start=(ct == 0), stop=(ct == CT - 1))
            last.then_inc(work_full, 1)
            pe.wait_ge(weights_loaded, 112)
            pe.wait_ge(ctx_loaded, CT * 16)
            pe.wait_ge(x_loaded, 32)
            pe.wait_ge(consts_loaded, 64)
            for g in range(2):
                for c in range(2):
                    pe.wait_ge(work_empty, PRO_ORDER["K", g, c])
                    k_piece(g, c, range(CT), None)
                pe.wait_ge(work_empty, PRO_ORDER["Q", g])
                q_piece(g, None)
                ip_piece(g, PRO_ORDER["Q", g], 1)
            units = iter(range(UNITS))
            for t in range(FULL - 1):
                pe.wait_ge(work_empty, PRO_ORDER["V", t])
                v_piece(t)
                if t == 0:
                    pe.wait_ge(stack_loaded[0], 192)
                for _ in range(3):
                    u = next(units, None)
                    if u is not None:
                        max_unit(0, 0, u, True)
            pe.wait_ge(cleared, 8)
            pe.wait_ge(work_empty, PRO_ORDER["NEG", 0])
            negative_piece(0)
            pe.wait_ge(ones_ready, 1)

            def body(b, first, last):
                plan = work_plan(first, last)
                for g in range(NG):
                    group_no = b * NG + g
                    units = iter(range(UNITS))

                    def next_units(n):
                        for _ in range(n):
                            u = next(units)
                            if u == 0:
                                nb = b + 1 if g < NG - 1 else b + 2
                                pe.wait_ge(stack_loaded[(g + 1) % NG], nb * 192)
                            max_unit(group_no + 1, g + 1, u, False)

                    pe.wait_ge(neg_loaded, (group_no + 1) * 16)
                    for kt in range(KT):
                        places = (0,) * 4 if last and g == NG - 1 else units_at(g, kt)
                        tiles = list(exps_of(kt))
                        for j in tiles[:2]:
                            exp_tile(group_no, g, kt, j, first and g == 0)
                        next_units(places[0])
                        if kt:
                            pv_tile(group_no, g, kt - 1)
                        elif g or not first:
                            pv_tile(group_no - 1, (g - 1) % NG, FULL)
                        next_units(places[1])
                        if kt == NEG_AT and not (last and g == NG - 1):
                            pe.wait_ge(work_empty, work_number(b, ("NEG", g + 1), first, last))
                            negative_piece(group_no + 1)
                        for j in tiles[2:]:
                            exp_tile(group_no, g, kt, j, first and g == 0)
                        next_units(places[2])
                        if (g, kt) in plan:
                            work(b, plan[g, kt], first, last, kt, g)
                        next_units(places[3])

            batches(pe, body)
            pv_tile(B * NG - 1, NG - 1, FULL)
            end = len(PRO) + FIRST_WORK + (B - 2) * LOOP_WORK + len(work_order(False, True))
            pe.wait_ge(o_packed, B * NG * 64)
            for t in range(QT):
                pe.wait_ge(work_empty, end + t)
                out_piece(t)

        @block.scalar
        def _(act):
            def copy(dst, src):
                return nc.scalar.activation(dst, src, ACT.Copy)

            def k_first_part(b, g, c, number):
                act.wait_ge(work_full, number + 1)
                if c == 0:
                    act.wait_ge(k_stored, (b * NG + g) * 32)
                copy(k_parts[:, 0, c * CHUNK:(c + 1) * CHUNK], work_bank[:, 0:CHUNK]).then_inc(k_high, 1)

            def q_copy(b, g, number):
                act.wait_ge(work_full, number + 1)
                act.wait_ge(q_step, (b * NG + g) * 4)
                copy(q_full[:, :], work_bank[:, 0:QHALF]).then_inc(work_empty, 1)

            def v_copy(b, t, number, reused):
                act.wait_ge(work_full, number + 1)
                if reused:
                    act.wait_ge(pv_done, (b * NG - 1) * KT + t + 1)
                v = v_ones[:, t, :].rearrange("p (h d) -> p h d", d=VW)
                w = work_bank[:, 0:D].rearrange("p (h d) -> p h d", d=DH)
                if t < FULL:
                    copy(v[:, :, 0:DH], w[:, :, :]).then_inc(work_empty, 1)
                else:
                    copy(v[0:TAILV, 0:HEADS:2, 0:DH], w[0:TAILV, 0:HEADS:2, :])
                    copy(v[TAIL:TAIL + TAILV, 1:HEADS:2, 0:DH], w[TAIL:TAIL + TAILV, 1:HEADS:2, :]).then_inc(work_empty, 1)

            def negative_copy(group_no, g, number, first_group):
                act.wait_ge(work_full, number + 1)
                if not first_group:
                    act.wait_ge(neg_loaded, group_no * 16)
                copy(neg_rows[:, :], work_bank[:, :].bitcast(BF16)[0:PARTS * UNITS // 2, 0:128]).then_inc(work_empty, 1)
                act.wait_ge(work_empty, number + 1)
                act.dma_start(q_stack[STACK:ROWS, SLOTS[g % NG], :, :], neg_rows[:, :]).then_inc(neg_loaded, 16)

            def exp_tile(group_no, kt, j, first_group):
                n = kt * GH + j
                act.wait_ge(scores_ready, group_no * EXPS + n + 1)
                if j == 0:
                    if kt == FULL:
                        if not first_group:
                            act.wait_ge(pv_done, group_no * KT)
                    elif kt >= 2:
                        act.wait_ge(pv_done, group_no * KT + kt - 1)
                    elif not first_group:
                        act.wait_ge(pv_done, group_no * KT + kt - 2)
                dst = probs[:, kt % 2, j, :] if kt < FULL else probs_tail[:, j, :]
                nc.scalar.activation(dst, exp_bank[:, n % 2, :], ACT.Exp, scale=SCALE).then_inc(probs_ready, 1)

            def o_copy(group_no):
                act.wait_ge(pv_done, (group_no + 1) * KT)
                act.wait_ge(o_packed, group_no * 64)
                copy(o_sum[:, :], pv_bank[:, :]).then_inc(o_read, 1)

            act.wait_ge(work_full, 1)
            copy(kip[:, :, :].rearrange("p g n -> p (g n)"), work_bank[:, 0:D]).then_inc(work_empty, 1)
            act.wait_ge(work_full, 2)
            copy(vip[:, 0:2, :].rearrange("p m n -> p (m n)"), work_bank[:, 0:128])
            copy(vip[0:64, 2, :], work_bank[0:64, 128:192]).then_inc(work_empty, 1)
            for g in range(2):
                for c in range(2):
                    k_first_part(0, g, c, PRO_ORDER["K", g, c])
                q_copy(0, g, PRO_ORDER["Q", g])
            act.wait_ge(cleared, 8)
            for t in range(FULL - 1):
                v_copy(0, t, PRO_ORDER["V", t], False)
            negative_copy(0, 0, PRO_ORDER["NEG", 0], True)

            def body(b, first, last):
                plan = work_plan(first, last)
                for g in range(NG):
                    group_no = b * NG + g
                    for kt in range(KT):
                        tiles = list(exps_of(kt))
                        for j in tiles[:2]:
                            exp_tile(group_no, kt, j, first and g == 0)
                        if kt == 0 and (g or not first):
                            o_copy(group_no - 1)
                        if kt == NEG_AT and not (last and g == NG - 1):
                            negative_copy(group_no + 1, g + 1, work_number(b, ("NEG", g + 1), first, last), False)
                        for j in tiles[2:]:
                            exp_tile(group_no, kt, j, first and g == 0)
                        if (g, kt) == (3, 1):
                            act.wait_ge(ip_step, b * 5 + 3)
                            nc.scalar.activation(s_ip[:, :, :], s_ip[:, :, :], ACT.Exp).then_inc(ip_exp, 1)
                        piece = plan.get((g, kt))
                        if piece is None:
                            continue
                        kind = piece[0]
                        if kind == "K":
                            if piece[3] == 1:
                                k_first_part(b, piece[1], piece[2], work_number(b, piece[:3], first, last))
                            continue
                        number = work_number(b, piece, first, last)
                        if kind == "Q":
                            q_copy(b, piece[1], number)
                        elif kind == "V":
                            if piece[1] >= FULL - 1:
                                v_copy(b, piece[1], number, not first)
                            else:
                                v_copy(b + 1, piece[1], number, True)
                        elif kind == "WA":
                            act.wait_ge(work_full, number + 1)
                            copy(wout[64:128, 3, :], work_bank[64:128, 0:D]).then_inc(work_empty, 1)
                        elif kind == "WB":
                            act.wait_ge(work_full, number + 1)
                            copy(wout[0:64, 3, :], work_bank[0:64, 0:D])
                            copy(wout[64:96, 2, :], work_bank[64:96, 0:D]).then_inc(work_empty, 1)
                        elif kind == "TA":
                            act.wait_ge(work_full, number + 1)
                            copy(o_t[:, 3, :], work_bank[:, :]).then_inc(work_empty, 1)
                        elif kind == "TB":
                            act.wait_ge(work_full, number + 1)
                            copy(o_t[64:96, 2, :], work_bank[64:96, :]).then_inc(work_empty, 1)

            batches(act, body)
            o_copy(B * NG - 1)

        @block.vector
        def _(dve):
            def k_remainder(b, g, c, number, reused=True):
                dve.wait_ge(k_high, (b * NG + g) * 2 + c + 1)
                if reused:
                    dve.wait_ge(k_split, (b * NG + g) * 2 + c - 1)
                nc.vector.tensor_tensor(k_rest[:, c, :], work_bank[:, 0:CHUNK], k_parts[:, 0, c * CHUNK:(c + 1) * CHUNK],
                                        ALU.subtract).then_inc(work_empty, 1)

            def ip_scale(g, number):
                dve.wait_ge(work_full, number + 1)
                src = work_bank[:, 0:128].rearrange("p (n f m) -> p n f m", n=2, f=2)
                for half in range(2):
                    last = nc.vector.tensor_scalar(
                        s_ip[:, half * 2:half * 2 + 2, (g % NG) * 32:(g % NG + 1) * 32], src[:, :, half, :], SCALE, None, ALU.mult)
                last.then_inc(work_empty, 1)

            def take_max(group_no, u):
                dve.wait_ge(max_scores, group_no * UNITS + u + 1)
                nc.vector.reduce_max(half_max[:, u:u + 1], max_bank[:, (u % 2) * 2:(u % 2) * 2 + 2, 0:CHUNK], AX.XY)\
                  .then_inc(max_taken, 1)

            def negative_parts(group_no):
                dve.wait_ge(max_taken, (group_no + 1) * UNITS)
                nc.vector.reduce_max(neg_max[:, :], half_max[:, :].rearrange("p (m f) -> p m f", f=2), AX.X, negate=True)\
                  .then_inc(neg_step, 1)
                dve.wait_ge(neg_step, group_no * 5 + 1)
                nc.vector.tensor_copy(neg_parts[:, 0, :], neg_max[:, :]).then_inc(neg_step, 1)
                dve.wait_ge(neg_step, group_no * 5 + 2)
                nc.vector.tensor_tensor(neg_rest[:, :], neg_max[:, :], neg_parts[:, 0, :], ALU.subtract).then_inc(neg_step, 1)
                dve.wait_ge(neg_step, group_no * 5 + 3)
                nc.vector.tensor_copy(neg_parts[:, 1, :], neg_rest[:, :]).then_inc(neg_step, 1)
                dve.wait_ge(neg_step, group_no * 5 + 4)
                nc.vector.tensor_tensor(neg_parts[:, 2, :], neg_rest[:, :], neg_parts[:, 1, :], ALU.subtract)\
                  .then_inc(neg_step, 1)

            def invert_sums(group_no):
                dve.wait_ge(sums_loaded, (group_no + 1) * 16)
                dve.wait_ge(recips_stored, group_no * 16)
                nc.vector.reciprocal(recips[:, :], sums[:, :]).then_inc(recips_ready, 1)

            def ip_softmax_1(b, number):
                scores = s_ip[:, :, :].rearrange("p q (h t) -> p q h t", t=IPT)
                m = mask[:, bass.ds(b, 1), :, :].rearrange("p o q t -> p (o q) t")
                dve.wait_ge(work_empty, number + 1)
                nc.vector.tensor_tensor(scores, scores, m.unsqueeze(2).to_broadcast([128, QT, HEADS, IPT]), ALU.add)\
                  .then_inc(ip_step, 1)
                dve.wait_ge(ip_step, b * 5 + 1)
                nc.vector.reduce_max(ip_max[:, :, :], scores, AX.X).then_inc(ip_step, 1)
                dve.wait_ge(ip_step, b * 5 + 2)
                nc.vector.tensor_tensor(scores, scores, ip_max[:, :, :].unsqueeze(3).to_broadcast([128, QT, HEADS, IPT]),
                                        ALU.subtract).then_inc(ip_step, 1)

            def ip_softmax_2(b):
                scores = s_ip[:, :, :].rearrange("p q (h t) -> p q h t", t=IPT)
                dve.wait_ge(ip_exp, b + 1)
                nc.vector.reduce_sum(ip_sum[:, :, :], scores, AX.X).then_inc(ip_exp_sum, 1)
                dve.wait_ge(ip_exp_sum, b + 1)
                nc.vector.reciprocal(ip_max[:, :, :], ip_sum[:, :, :]).then_inc(ip_step, 1)
                dve.wait_ge(ip_step, b * 5 + 4)
                nc.vector.tensor_tensor(p_ip[:, :, :].rearrange("p q (h t) -> p q h t", t=IPT), scores,
                                        ip_max[:, :, :].unsqueeze(3).to_broadcast([128, QT, HEADS, IPT]), ALU.mult)\
                  .then_inc(ip_step, 1)

            def out_add(b, t, number):
                dve.wait_ge(work_full, number + 1)
                if t == 0:
                    dve.wait_ge(residual_loaded, b * 16)
                dve.wait_ge(out_stored[t % 2], ((b - 1) * 2 + t // 2) * 16)
                nc.vector.tensor_tensor(out_sb[:, t % 2, :], work_bank[:, 0:D], xres[:, t, :], ALU.add)\
                  .then_inc(work_empty, 1)

            nc.vector.memset(pv_bank[:, :], 0.0).then_inc(cleared, 1)
            nc.vector.memset(v_ones[:, :, :], 0.0).then_inc(mask_step, 1)
            dve.wait_ge(mask_step, 1)
            v = v_ones[:, :, :].rearrange("p t (h d) -> p t h d", d=VW)
            nc.vector.memset(v[:, 0:FULL, :, DH], 1.0).then_inc(cleared, 1)
            nc.vector.memset(v[0:TAILV, FULL, 0:HEADS:2, DH], 1.0).then_inc(cleared, 1)
            nc.vector.memset(v[TAIL:TAIL + TAILV, FULL, 1:HEADS:2, DH], 1.0).then_inc(cleared, 1)
            nc.vector.memset(o_t[96:97, 2, :], 1.0).then_inc(cleared, 1)

            dve.wait_ge(consts_loaded, 64)
            nc.vector.tensor_copy(ident_b[:, :], ident_f[:, :]).then_inc(cleared, 1)

            nc.vector.memset(neg_parts[:, :, :], 0.0).then_inc(cleared, 1)
            nc.vector.memset(zero[:, :], 0.0).then_inc(cleared, 1)

            tests = ((0, 0, ALU.is_ge), (1, 1, ALU.is_ge), (0, 2, ALU.is_le), (1, 3, ALU.is_le))
            step = 1
            for n, (axis, corner, op) in enumerate(tests):
                place = grid_sb[:, axis, :].unsqueeze(1).unsqueeze(3).to_broadcast([128, B, QT, 4])
                limit = box[:, :, :, corner].unsqueeze(2).to_broadcast([128, B, QT, 4])
                nc.vector.tensor_tensor((cmp if n else inside)[:, :, :, :], place, limit, op).then_inc(mask_step, 1)
                step += 1
                dve.wait_ge(mask_step, step)
                if n:
                    nc.vector.tensor_tensor(inside[:, :, :, :], inside[:, :, :, :], cmp[:, :, :, :], ALU.mult)\
                      .then_inc(mask_step, 1)
                    step += 1
                    dve.wait_ge(mask_step, step)
            nc.vector.tensor_scalar(mask[:, :, :, IPT // 2:IPT], inside[:, :, :, :], -NEG, NEG, ALU.mult, ALU.add)\
              .then_inc(mask_step, 1)
            nc.vector.reduce_max(outside[:, :, :], inside[:, :, :, :], AX.X).then_inc(mask_step, 1)
            dve.wait_ge(mask_step, step + 2)
            nc.vector.tensor_scalar(mask[:, :, :, 0:IPT // 2], outside[:, :, :].unsqueeze(3).to_broadcast([128, B, QT, 4]),
                                    NEG, None, ALU.mult).then_inc(mask_step, 1)
            dve.wait_ge(mask_step, step + 3)

            for g in range(2):
                for c in range(2):
                    k_remainder(0, g, c, PRO_ORDER["K", g, c], g > 0)
                ip_scale(g, PRO_ORDER["IP", g])
            for u in range(UNITS):
                take_max(0, u)
            negative_parts(0)

            def body(b, first, last):
                plan = work_plan(first, last)
                for g in range(NG):
                    group_no = b * NG + g
                    units = iter(range(UNITS))
                    for kt in range(KT):
                        places = (0,) * 4 if last and g == NG - 1 else units_at(g, kt)
                        for _ in range(sum(places)):
                            u = next(units)
                            take_max(group_no + 1, u)
                            if u == UNITS - 1:
                                negative_parts(group_no + 1)
                        piece = plan.get((g, kt))
                        if kt == 1 and (g or not first):
                            invert_sums(group_no - 1)
                        if piece is not None and (piece[0] != "K" or piece[3] == 1):
                            number = work_number(b, piece[:3] if piece[0] == "K" else piece, first, last)
                            if piece[0] == "K":
                                k_remainder(b, piece[1], piece[2], number)
                            elif piece[0] == "IP":
                                ip_scale(piece[1], number)
                            elif piece[0] == "OUT":
                                out_add(b, piece[1], number)
                        if (g, kt) == (3, 0):
                            ip_softmax_1(b, work_number(b, ("IP", 4), first, last))
                        if (g, kt) == (3, 2):
                            ip_softmax_2(b)

            batches(dve, body)
            end = len(PRO) + FIRST_WORK + (B - 2) * LOOP_WORK + len(work_order(False, True))
            invert_sums(B * NG - 1)
            for t in range(QT):
                out_add(B, t, end + t)

        @block.gpsimd
        def _(pool):
            def split_k(b, g, c, number):
                pool.wait_ge(work_empty, number + 1)
                part = k_parts[:, :, c * CHUNK:(c + 1) * CHUNK]
                nc.gpsimd.tensor_tensor(part[:, 1, :], k_rest[:, c, :], zero[:, :].to_broadcast([128, CHUNK]), ALU.add).then_inc(k_mid, 1)
                pool.wait_ge(k_mid, (b * NG + g) * 2 + c + 1)
                nc.gpsimd.tensor_tensor(part[:, 2, :], k_rest[:, c, :], part[:, 1, :], ALU.subtract).then_inc(k_split, 1)

            def split_q(b, g, number):
                done = (b * NG + g) * 4
                pool.wait_ge(work_empty, number + 1)
                pool.wait_ge(q_stored, (b * NG + g) * 32)
                nc.gpsimd.tensor_tensor(q_parts[:, 0, :], q_full[:, :], zero[:, :].to_broadcast([128, QHALF]), ALU.add).then_inc(q_step, 1)
                pool.wait_ge(q_step, done + 1)
                nc.gpsimd.tensor_tensor(q_rest[:, :], q_full[:, :], q_parts[:, 0, :], ALU.subtract).then_inc(q_step, 1)
                pool.wait_ge(q_step, done + 2)
                nc.gpsimd.tensor_tensor(q_parts[:, 1, :], q_rest[:, :], zero[:, :].to_broadcast([128, QHALF]), ALU.add).then_inc(q_step, 1)
                pool.wait_ge(q_step, done + 3)
                nc.gpsimd.tensor_tensor(q_parts[:, 2, :], q_rest[:, :], q_parts[:, 1, :], ALU.subtract).then_inc(q_step, 1)

            def own_k(b):
                src = kip[:, :, bass.ds(b * IPT, IPT)].unsqueeze(2).to_broadcast([128, NG, 8, IPT])
                nc.gpsimd.tensor_tensor(kip_own[:, :, :, :], src,
                                        own[:, :].unsqueeze(1).unsqueeze(3).to_broadcast([128, NG, 8, IPT]), ALU.mult)\
                  .then_inc(kip_ready, 1)

            def own_v(b):
                src = vip[:, :, bass.ds(b * IPT, IPT)]
                nc.gpsimd.tensor_tensor(vip_own[:, 0:2, :, :], src[:, 0:2, :].unsqueeze(2).to_broadcast([128, 2, 8, IPT]),
                                        own[:, :].unsqueeze(1).unsqueeze(3).to_broadcast([128, 2, 8, IPT]), ALU.mult)
                nc.gpsimd.tensor_tensor(vip_own[0:64, 2, 0:GH, :], src[0:64, 2, :].unsqueeze(1).to_broadcast([64, GH, IPT]),
                                        own[0:64, 0:GH].unsqueeze(2).to_broadcast([64, GH, IPT]), ALU.mult).then_inc(vip_ready, 1)

            def scale_o(group_no):
                pool.wait_ge(r_wide_loaded, (group_no + 1) * 16)
                nc.gpsimd.tensor_tensor(o_sum[:, :], o_sum[:, :], r_wide[:, :], ALU.mult).then_inc(o_scaled, 1)

            pool.dma_start(own[:, :], own_rows).then_inc(consts_loaded, 16)
            pool.dma_start(ident_f[:, :], ident).then_inc(consts_loaded, 16)
            pool.dma_start(grid_sb[:, :, :], grid).then_inc(consts_loaded, 16)
            pool.dma_start(box[:, :, :, :].rearrange("p b m k -> p (b m k)"),
                           boxes.rearrange("b m k -> (b m k)").partition_broadcast(128)).then_inc(consts_loaded, 16)
            pool.wait_ge(consts_loaded, 64)
            pool.wait_ge(cleared, 8)
            pool.wait_ge(work_empty, 2)
            own_k(0)
            for g in range(2):
                for c in range(2):
                    split_k(0, g, c, PRO_ORDER["K", g, c])
                split_q(0, g, PRO_ORDER["Q", g])
            pool.wait_ge(q_step, 8)
            nc.gpsimd.memset(k_stack[STACK:ROWS, :, :, :], 1.0).then_inc(ones_ready, 1)
            pool.wait_ge(ones_ready, 1)

            def body(b, first, last):
                number = lambda piece: work_number(b, piece, first, last)
                for g in range(NG):
                    if g or not first:
                        scale_o(b * NG + g - 1)
                    for piece in SPLITS[g] if g < 3 or not last else ():
                        if piece[0] == "K":
                            split_k(b, piece[1], piece[2], number(piece))
                        else:
                            split_q(b, piece[1], number(piece))
                    if g == 1:
                        own_v(b)
                    if g == 2 and not last:
                        pool.wait_ge(work_full, number(("IP", 4)) + 1)
                        own_k(b + 1)

            batches(pool, body)
            scale_o(B * NG - 1)


def kernel(x, ctx_2048, fside_Bx4x4_0, L0_xattn_w_q, L0_xattn_w_k, L0_xattn_w_v, L0_xattn_w_k_ip, L0_xattn_w_v_ip,
           L0_xattn_w_out, L0_xattn_b_out):
    import concourse.bacc as bacc
    from concourse.bass_utils import run_bass_kernel_spmd

    x, ctx = np.asarray(x), np.asarray(ctx_2048)
    text = np.concatenate([ctx[:, :TEXT], ctx[:, :KEYS - TEXT]], axis=1)
    q = np.arange(S)
    step_x = (np.arange(GRID_W, dtype=np.float32) / np.float32(GRID_W - 1)).astype(np.float32)
    step_y = (np.arange(GRID_H, dtype=np.float32) / np.float32(GRID_H - 1)).astype(np.float32)
    places = np.stack([step_x[q % GRID_W], step_y[q // GRID_W]])
    arrays = {
        "x": x,
        "x_t": x.transpose(0, 2, 1),
        "ctx_t": text.transpose(0, 2, 1),
        "ctx_ip_t": ctx[:, TEXT:].transpose(2, 0, 1).reshape(C, B * IPT),
        "boxes": np.asarray(fside_Bx4x4_0),
        "grid": places.reshape(2, QT, 128).transpose(2, 0, 1),
        "own_rows": (np.arange(128)[:, None] // DH == np.arange(8)[None, :]).astype(np.float32),
        "ident": np.eye(128, dtype=np.float32),
        "w_q": L0_xattn_w_q, "w_k": L0_xattn_w_k, "w_v": L0_xattn_w_v, "w_k_ip": L0_xattn_w_k_ip,
        "w_v_ip": L0_xattn_w_v_ip, "w_out": L0_xattn_w_out, "b_out": L0_xattn_b_out,
    }
    nc = bacc.Bacc("TRN2", target_bir_lowering=False, num_devices=1)
    feeds, args = {}, []
    for name, a in arrays.items():
        a = np.ascontiguousarray(a)
        feeds[f"in_{name}"] = a
        args.append(nc.dram_tensor(f"in_{name}", a.shape, mybir.dt.from_np(a.dtype), kind="ExternalInput").ap())
    out = nc.dram_tensor("out", (B, S, D), FP32, kind="ExternalOutput").ap()
    cross_attention(nc, *args, out)
    r = run_bass_kernel_spmd(nc, [feeds], core_ids=[0])
    return r.results[0]["out"]
```

```python
import numpy as np
import concourse.bass as bass
from concourse import mybir
from contextlib import ExitStack

FP32 = mybir.dt.float32
BF16 = mybir.dt.bfloat16
ALU = mybir.AluOpType
ACT = mybir.ActivationFunctionType
AX = mybir.AxisListType

B, S, D, C = 8, 512, 320, 512
HEADS, DH = 20, 16
TOKENS = 1601
IPT = 8
TEXT = TOKENS - IPT
KEYS = 1600
GH = 4
NG = HEADS // GH
GR = GH * DH
CT = C // 128
QT = S // 128
FULL = KEYS // 128
TAIL = KEYS - FULL * 128
TAILV = TEXT - FULL * 128
KT = FULL + 1
HALF = KEYS // 2
CHUNK = HALF // 2
QHALF = S // 2
VW = DH + 1
PARTS = 3
RUNS = ((0, 3), (3, 2), (5, 1))
STACK = 6 * DH
ROWS = STACK + PARTS
SLOTS = (0, 1, 2, 3, 2)
EXPS = FULL * GH + GH // 2
UNITS = GH * QT * 2
SCALE = float(DH) ** -0.5
NEG = -10000.0
GRID_W, GRID_H = 32, 16


V_EARLY = 6


TURNS = (range(CT // 2), range(CT // 2, CT), range(CT))


def work_plan(first, last):
    turns = {("Q", 2): (0, 0), ("K", 2, 0): (0, 1, 2), ("K", 2, 1): (0, 3, 4), ("IP", 2): (0, 5),
             ("K", 3, 0): (1, 0, 1), ("K", 3, 1): (1, 2, 3), ("Q", 3): (1, 4), ("IP", 3): (1, 5), ("K", 4, 0): (1, 12),
             ("K", 4, 1): (2, 0, 2), ("Q", 4): (2, 4), ("IP", 4): (2, 6), ("WA",): (2, 8), ("WB",): (2, 10),
             ("TA",): (3, 4), ("TB",): (3, 10)}
    turns.update({("V", t): (0, t) for t in range(V_EARLY, KT)})
    if not first:
        turns.update({("OUT", 0): (1, 6, 7), ("OUT", 1): (1, 8, 9), ("OUT", 2): (1, 10), ("OUT", 3): (1, 11)})
    if not last:
        turns.update({("K", 5, 0): (2, 12), ("K", 5, 1): (3, 0, 2), ("Q", 5): (3, 3), ("IP", 5): (3, 5), ("Q", 6): (3, 6),
                      ("IP", 6): (3, 8), ("K", 6, 0): (3, 12), ("K", 6, 1): (4, 0, 1)})
        turns.update({("V", t): (4, 2 * t + 2, 2 * t + 3) for t in range(V_EARLY - 1)})
        turns["V", V_EARLY - 1] = (4, KT - 1)
    plan = {}
    for piece, (g, *kts) in turns.items():
        for n, kt in enumerate(kts):
            assert (g, kt) not in plan
            plan[g, kt] = (piece, n if len(kts) == 2 else 2)
    return plan


SPLITS = ((("Q", 2), ("K", 2, 0), ("K", 2, 1)), (("K", 3, 0), ("K", 3, 1), ("Q", 3)), (("K", 4, 0), ("K", 4, 1), ("Q", 4)),
          (("K", 5, 0), ("K", 5, 1), ("Q", 5), ("Q", 6)), (("K", 6, 0), ("K", 6, 1)))
SCALE_AT = (0, 3, 1, 2, 2)
NEG_AT = FULL
INVERT_AT = (2, 2, 2, 3, 2)


def work_order(first, last):
    plan, order = work_plan(first, last), {}
    for g in range(NG):
        for kt in range(KT):
            if kt == NEG_AT and not (last and g == NG - 1):
                order["NEG", g + 1] = len(order)
            piece, turn = plan.get((g, kt), (None, None))
            if piece is not None and turn != 1:
                order[piece] = len(order)
    return order


PRO = [("KIP",), ("VIP",)] + [p for g in (0, 1) for p in (("K", g, 0), ("K", g, 1), ("Q", g), ("IP", g))]
PRO += [("V", t) for t in range(V_EARLY)] + [("NEG", 0)]
PRO_ORDER = {p: n for n, p in enumerate(PRO)}
FIRST_WORK = len(work_order(True, False))
LOOP_WORK = len(work_order(False, False))


UNITS_AT = ((3, 3, 3, 3, 3, 3, 3, 3, 3, 2, 2, 1), (3, 3, 3, 3, 3, 3, 3, 3, 3, 2, 2, 1), (3, 2, 3, 2, 3, 3, 3, 3, 3, 3, 3, 1),
            (0, 0, 3, 4, 4, 3, 4, 3, 4, 3, 3, 1), (3, 3, 3, 3, 3, 3, 3, 3, 3, 2, 2, 1))
PLACES = ((0, 0, 0, 0), (1, 0, 0, 0), (1, 0, 1, 0), (1, 1, 1, 0), (1, 1, 1, 1), (1, 1, 1, 2))
LAST_PLACES = ((0, 0, 0, 0), (1, 0, 0, 0), (1, 1, 0, 0), (1, 1, 1, 0), (1, 1, 1, 1))
assert all(sum(u) == UNITS for u in UNITS_AT)


def units_at(g, kt):
    if kt >= len(UNITS_AT[g]):
        return PLACES[0]
    return (LAST_PLACES if kt == len(UNITS_AT[g]) - 1 else PLACES)[UNITS_AT[g][kt]]


def exps_of(kt):
    return range(GH) if kt < FULL else range(GH // 2)


def cross_attention(nc, x, x_t, ctx_t, ctx_ip_t, boxes, grid, own_k_rows, own_v_rows, ident, w_q, w_k, w_v, w_k_ip, w_v_ip,
                    w_out, b_out, out):
    scratch_k = nc.dram_tensor("scratch_k", (NG, PARTS, GR, KEYS), BF16, kind="Internal").ap()
    scratch_q = nc.dram_tensor("scratch_q", (NG, PARTS, GR, S), BF16, kind="Internal").ap()
    scratch_r = nc.dram_tensor("scratch_r", (GH, S), FP32, kind="Internal").ap()

    ctx = ExitStack()
    with ctx:
        def sb(name, shape, dt=FP32):
            return ctx.enter_context(nc.sbuf_tensor(name, shape, dt))

        def sem(name):
            return ctx.enter_context(nc.semaphore(name))

        wq = sb("wq", [128, 3, D])
        wk = sb("wk", [128, CT, D])
        wv = sb("wv", [128, CT, D])
        wout = sb("wout", [128, 4, D])
        own_k_sb = sb("own_k_sb", [128, 8])
        own_v_sb = sb("own_v_sb", [128, 8])
        ident_f = sb("ident_f", [128, 128])
        ident_b = sb("ident_b", [128, 128], BF16)
        grid_sb = sb("grid_sb", [128, 2, QT])
        box = sb("box", [128, B, 4, 4])
        inside = sb("inside", [128, B, QT, 4])
        cmp = sb("cmp", [128, B, QT, 4])
        outside = sb("outside", [128, B, QT])
        mask = sb("mask", [128, B, QT, IPT])
        ctxt = sb("ctxt", [128, CT, KEYS])
        xt = sb("xt", [128, 3, S])
        xres = sb("xres", [128, QT, D])
        k_parts = sb("k_parts", [128, PARTS, HALF], BF16)
        k_rest = sb("k_rest", [128, 2, CHUNK])
        q_full = sb("q_full", [128, QHALF])
        q_rest = sb("q_rest", [128, QHALF])
        q_parts = sb("q_parts", [128, PARTS, QHALF], BF16)
        k_stack = sb("k_stack", [128, 4, GH, KEYS], BF16)
        q_stack = sb("q_stack", [128, NG, GH, S], BF16)
        v_ones = sb("v_ones", [128, KT, HEADS * VW])
        probs = sb("probs", [128, 2, GH, S])
        probs_tail = sb("probs_tail", [128, GH // 2, S])
        half_max = sb("half_max", [128, UNITS])
        neg_max = sb("neg_max", [128, UNITS // 2])
        neg_rest = sb("neg_rest", [128, UNITS // 2])
        neg_parts = sb("neg_parts", [128, 8, UNITS // 2], BF16)
        neg_rows = sb("neg_rows", [PARTS * UNITS // 2, 128], BF16)
        zero = sb("zero", [128, 1])
        o_sum = sb("o_sum", [128, S])
        sums = sb("sums", [128, GH * S // 128])
        recips = sb("recips", [128, GH * S // 128])
        r_wide = sb("r_wide", [128, S])
        o_t = sb("o_t", [128, 4, S])
        out_sb = sb("out_sb", [128, 2, D])
        kip = sb("kip", [128, NG, B * IPT])
        vip = sb("vip", [128, 3, B * IPT])
        kip_own = sb("kip_own", [128, NG, 8, IPT])
        vip_own = sb("vip_own", [128, 3, 8, IPT])
        s_ip = sb("s_ip", [128, QT, HEADS * IPT])
        p_ip = sb("p_ip", [128, QT, HEADS * IPT])
        ip_max = sb("ip_max", [128, QT, HEADS])
        ip_sum = sb("ip_sum", [128, QT, HEADS])
        early = probs[:, :, :, :].rearrange("p a h n -> p (a h n)")
        wk_ip = early[:, 0:CT * D].rearrange("p (c n) -> p c n", c=CT)
        wv_ip = early[:, CT * D:2 * CT * D].rearrange("p (c n) -> p c n", c=CT)
        ctx_ip = early[:, 2 * CT * D:2 * CT * D + CT * B * IPT].rearrange("p (c n) -> p c n", c=CT)

        exp_bank = ctx.enter_context(nc.psum_tensor("exp_bank", [128, 2, 512], FP32))
        max_bank = ctx.enter_context(nc.psum_tensor("max_bank", [128, 4, 512], FP32))
        pv_bank = ctx.enter_context(nc.psum_tensor("pv_bank", [128, 512], FP32))
        work_bank = ctx.enter_context(nc.psum_tensor("work_bank", [128, 512], FP32))

        weights_ip_loaded = sem("weights_ip_loaded")
        weights_loaded = sem("weights_loaded")
        consts_loaded = sem("consts_loaded")
        ctx_loaded = sem("ctx_loaded")
        x_loaded = sem("x_loaded")
        residual_loaded = sem("residual_loaded")
        cleared = sem("cleared")
        mask_step = sem("mask_step")
        k_high = sem("k_high")
        k_mid = sem("k_mid")
        k_split = sem("k_split")
        k_stored = sem("k_stored")
        q_step = sem("q_step")
        q_stored = sem("q_stored")
        stack_loaded = [sem(f"stack_loaded{g}") for g in range(NG)]
        scores_ready = sem("scores_ready")
        probs_ready = sem("probs_ready")
        pv_done = sem("pv_done")
        max_scores = sem("max_scores")
        max_taken = sem("max_taken")
        neg_step = sem("neg_step")
        neg_loaded = sem("neg_loaded")
        o_read = sem("o_read")
        sums_loaded = sem("sums_loaded")
        recips_ready = sem("recips_ready")
        recips_stored = sem("recips_stored")
        r_wide_loaded = sem("r_wide_loaded")
        o_scaled = sem("o_scaled")
        o_packed = sem("o_packed")
        kip_ready = sem("kip_ready")
        vip_ready = sem("vip_ready")
        ip_step = sem("ip_step")
        ip_exp = sem("ip_exp")
        ip_exp_sum = sem("ip_exp_sum")
        ones_ready = sem("ones_ready")
        work_full = sem("work_full")
        work_empty = sem("work_empty")
        out_stored = [sem(f"out_stored{i}") for i in range(2)]

        def work_number(b, piece, first, last):
            local = work_order(first, last)[piece]
            if first:
                return len(PRO) + local
            return b * LOOP_WORK + (len(PRO) + FIRST_WORK - LOOP_WORK + local)

        def batches(eng, body):
            body(0, True, False)
            with eng.Fori(1, B - 1) as b:
                body(b, False, False)
            body(B - 1, False, True)

        block = ctx.enter_context(nc.Block())

        @block.sync
        def _(sp):
            def store_k(b, g):
                sp.wait_ge(k_split, (b * NG + g) * 2 + 2)
                for half in range(2):
                    sp.dma_start(scratch_k[g % NG, :, :, half * HALF:(half + 1) * HALF].rearrange("a r n -> r a n"),
                                 k_parts[half * GR:(half + 1) * GR, :, :]).then_inc(k_stored, 16)

            def store_q(b, g):
                sp.wait_ge(q_step, (b * NG + g) * 4 + 4)
                for half in range(2):
                    sp.dma_start(scratch_q[g % NG, :, :, half * QHALF:(half + 1) * QHALF].rearrange("a r n -> r a n"),
                                 q_parts[half * GR:(half + 1) * GR, :, :]).then_inc(q_stored, 16)

            def q_slot_free(b, g, early_batch):
                if not early_batch:
                    sp.wait_ge(scores_ready, (b * NG + g - NG + 1) * EXPS)

            def slot_free(b, g, early_batch):
                if g == 4:
                    sp.wait_ge(scores_ready, (b * NG + g - 1) * EXPS)
                elif g == 2:
                    if not early_batch:
                        sp.wait_ge(scores_ready, (b * NG + g - 2) * EXPS)
                elif not early_batch:
                    sp.wait_ge(scores_ready, (b * NG + g - NG + 1) * EXPS)

            def load_k(b, g):
                sp.wait_ge(k_stored, (b * NG + g + 1) * 32)
                for part, (block, count) in enumerate(RUNS):
                    src = scratch_k[g % NG, part].rearrange("(i h) n -> i (h n)", i=DH)
                    sp.dma_start(k_stack[block * DH:(block + count) * DH, SLOTS[g % NG], :, :].rearrange("p h n -> p (h n)"),
                                 src.unsqueeze(0).to_broadcast([count, DH, GH * KEYS]))\
                      .then_inc(stack_loaded[g % NG], 16)

            def load_q(b, g):
                sp.wait_ge(q_stored, (b * NG + g + 1) * 32)
                for block, count in RUNS:
                    sp.dma_start(q_stack[block * DH:(block + count) * DH, g % NG, :, :].rearrange("p h n -> p (h n)"),
                                 scratch_q[g % NG, 0:count].rearrange("a (i h) n -> (a i) (h n)", i=DH))\
                      .then_inc(stack_loaded[g % NG], 16)

            def stack_group(b, g, early_batch):
                store_k(b, g)
                slot_free(b, g, early_batch)
                load_k(b, g)
                store_q(b, g)
                q_slot_free(b, g, early_batch)
                load_q(b, g)

            def load_ctx(b):
                for c in range(CT):
                    sp.dma_start(ctxt[:, c, :], ctx_t[b, c * 128:(c + 1) * 128, :]).then_inc(ctx_loaded, 16)

            def load_x(b):
                sp.dma_start(xt[:, 0:2, :], x_t[b, 0:256, :].rearrange("(c p) n -> p c n", p=128)).then_inc(x_loaded, 16)
                sp.dma_start(xt[0:64, 2, :], x_t[b, 256:D, :]).then_inc(x_loaded, 16)

            def normalise(group_no):
                sp.wait_ge(o_read, group_no + 1)
                sp.dma_start(sums[:, :], o_sum[DH:128:32, :]).then_inc(sums_loaded, 16)
                sp.wait_ge(recips_ready, group_no + 1)
                sp.dma_start(scratch_r.rearrange("h (c n) -> (h c) n", n=GH * S // 128), recips[:, :])\
                  .then_inc(recips_stored, 16)
                sp.wait_ge(recips_stored, (group_no + 1) * 16)
                sp.dma_start(r_wide[:, :], scratch_r.unsqueeze(1).to_broadcast([GH, 32, S])).then_inc(r_wide_loaded, 16)

            def pack(group_no, g, out_done):
                sp.wait_ge(o_scaled, group_no + 1)
                if out_done is not None:
                    sp.wait_ge(work_full, out_done + 1)
                for h in range(GH):
                    row = (g % 2) * GR + h * DH
                    sp.dma_start(o_t[row:row + DH, g // 2, :], o_sum[h * 32:h * 32 + DH, :]).then_inc(o_packed, 16)

            def store_out(b, t, number):
                sp.wait_ge(work_empty, number + 1)
                sp.dma_start(out[b, t * 128:(t + 1) * 128, :], out_sb[:, t % 2, :]).then_inc(out_stored[t % 2], 16)

            sp.dma_start(ctx_ip, ctx_ip_t.rearrange("(c p) n -> p c n", p=128)).then_inc(weights_ip_loaded, 16)
            sp.dma_start(wk_ip, w_k_ip.rearrange("(c p) n -> p c n", p=128)).then_inc(weights_ip_loaded, 16)
            sp.dma_start(wv_ip, w_v_ip.rearrange("(c p) n -> p c n", p=128)).then_inc(weights_ip_loaded, 16)
            sp.dma_start(wk[:, :, :], w_k.rearrange("(c p) n -> p c n", p=128)).then_inc(weights_loaded, 16)
            load_ctx(0)
            load_x(0)
            sp.dma_start(wq[:, 0:2, :], w_q[0:256, :].rearrange("(c p) n -> p c n", p=128)).then_inc(weights_loaded, 16)
            sp.dma_start(wq[0:64, 2, :], w_q[256:D, :]).then_inc(weights_loaded, 16)
            sp.dma_start(wv[:, :, :], w_v.rearrange("(c p) n -> p c n", p=128)).then_inc(weights_loaded, 16)
            sp.dma_start(wout[:, 0:2, :], w_out[0:256, :].rearrange("(c p) n -> p c n", p=128)).then_inc(weights_loaded, 16)
            sp.dma_start(wout[0:64, 2, :], w_out[256:D, :]).then_inc(weights_loaded, 16)
            sp.dma_start(wout[96:97, 2, :], b_out.unsqueeze(0)).then_inc(weights_loaded, 16)
            stack_group(0, 0, True)
            stack_group(0, 1, True)

            def body(b, first, last):
                number = lambda piece: work_number(b, piece, first, last)
                for g in range(NG):
                    group_no = b * NG + g
                    if g == 0 and not first:
                        sp.dma_start(xres[:, :, :], x[b - 1].rearrange("(t p) d -> p t d", p=128))\
                          .then_inc(residual_loaded, 16)
                    if g == 3:
                        slot_free(b, 4, first)
                        load_k(b, 4)
                    if g or not first:
                        normalise(group_no - 1)
                    if g == 1:
                        stack_group(b, 3, first)
                        if not first:
                            for t in range(QT):
                                store_out(b - 1, t, number(("OUT", t)))
                        pack(group_no - 1, 0, None if first else number(("OUT", QT - 1)))
                    elif g or not first:
                        pack(group_no - 1, (g - 1) % NG, None)
                    if g == 0:
                        stack_group(b, 2, first)
                    elif g == 2:
                        store_k(b, 4)
                        if not last:
                            sp.wait_ge(work_full, number(("K", 4, 1)) + 1)
                            load_ctx(b + 1)
                        store_q(b, 4)
                        q_slot_free(b, 4, first)
                        load_q(b, 4)
                        if not last:
                            sp.wait_ge(work_full, number(("Q", 4)) + 1)
                            load_x(b + 1)
                    elif g > 2 and not last:
                        stack_group(b, g + 2, False)

            batches(sp, body)
            end = len(PRO) + FIRST_WORK + (B - 2) * LOOP_WORK + len(work_order(False, True))
            sp.dma_start(xres[:, :, :], x[B - 1].rearrange("(t p) d -> p t d", p=128)).then_inc(residual_loaded, 16)
            normalise(B * NG - 1)
            pack(B * NG - 1, NG - 1, None)
            for t in range(QT):
                store_out(B - 1, t, end + t)
            for i in range(2):
                sp.wait_ge(out_stored[i], B * QT // 2 * 16)

        @block.tensor
        def _(pe):
            def k_piece(g, c, ct_range):
                for ct in ct_range:
                    for half in range(2):
                        keys = half * HALF + c * CHUNK
                        last = nc.tensor.matmul(work_bank[half * GR:(half + 1) * GR, 0:CHUNK],
                                                wk[:, ct, (g % NG) * GR:(g % NG + 1) * GR], ctxt[:, ct, keys:keys + CHUNK],
                                                start=(ct == 0), stop=(ct == CT - 1))
                if ct_range[-1] == CT - 1:
                    last.then_inc(work_full, 1)

            def q_piece(g):
                for ct, rows in enumerate((128, 128, 64)):
                    for half in range(2):
                        last = nc.tensor.matmul(work_bank[half * GR:(half + 1) * GR, 0:QHALF],
                                                wq[0:rows, ct, (g % NG) * GR:(g % NG + 1) * GR],
                                                xt[0:rows, ct, half * QHALF:(half + 1) * QHALF],
                                                start=(ct == 0), stop=(ct == 2))
                last.then_inc(work_full, 1)

            def ip_piece(g, q_number, kip_count):
                pe.wait_ge(work_empty, q_number + 1)
                pe.wait_ge(kip_ready, kip_count)
                for n in range(2):
                    last = nc.tensor.matmul(work_bank[:, n * 64:(n + 1) * 64], q_full[:, n * 128:(n + 1) * 128],
                                            kip_own[:, g % NG, :, :].rearrange("p h t -> p (h t)"), start=True, stop=True)
                last.then_inc(work_full, 1)

            def v_piece(t, ct_range):
                if t < FULL:
                    for ct in ct_range:
                        last = nc.tensor.matmul(work_bank[:, 0:D], ctxt[:, ct, t * 128:(t + 1) * 128], wv[:, ct, :],
                                                start=(ct == 0), stop=(ct == CT - 1))
                else:
                    for ct in ct_range:
                        for odd in range(2):
                            last = nc.tensor.matmul(work_bank[odd * TAIL:odd * TAIL + TAILV, 0:D],
                                                    ctxt[:, ct, FULL * 128:TEXT], wv[:, ct, :],
                                                    start=(ct == 0), stop=(ct == CT - 1))
                if ct_range[-1] == CT - 1:
                    last.then_inc(work_full, 1)

            def out_piece(t, k_range):
                for k in k_range:
                    rows = (128, 128, 97, 128)[k]
                    last = nc.tensor.matmul(work_bank[:, 0:D], o_t[0:rows, k, t * 128:(t + 1) * 128], wout[0:rows, k, :],
                                            start=(k == 0), stop=(k == 3))
                if k_range[-1] == 3:
                    last.then_inc(work_full, 1)

            def negative_piece(group_no):
                pe.wait_ge(neg_step, group_no * 5 + 5)
                nc.tensor.transpose(work_bank[:, :].bitcast(BF16)[:, 0:128],
                                    neg_parts[:, :, :].rearrange("p a m -> p (a m)"), ident_b[:, :]).then_inc(work_full, 1)

            def work(b, piece, turn, first, last):
                number = lambda p: work_number(b, p, first, last)
                kind = piece[0]
                if turn != 1:
                    pe.wait_ge(work_empty, number(piece))
                if kind == "K":
                    if piece == ("K", 5, 0):
                        pe.wait_ge(ctx_loaded, (b + 2) * CT * 16)
                    k_piece(piece[1], piece[2], TURNS[turn])
                elif kind == "Q":
                    if piece[1] == 5:
                        pe.wait_ge(x_loaded, (b + 2) * 32)
                    q_piece(piece[1])
                elif kind == "IP":
                    ip_piece(piece[1], number(("Q", piece[1])), b + (2 if piece[1] >= NG else 1))
                elif kind == "V":
                    v_piece(piece[1], TURNS[turn])
                elif kind == "OUT":
                    if piece[1] == 0:
                        pe.wait_ge(o_packed, b * NG * 64)
                    out_piece(piece[1], TURNS[turn])
                elif kind == "WA":
                    pe.wait_ge(vip_ready, b + 1)
                    nc.tensor.matmul(work_bank[64:128, 0:D], vip_own[:, 1, :, :].rearrange("p h t -> p (h t)"),
                                     wout[:, 1, :], start=True, stop=True).then_inc(work_full, 1)
                elif kind == "WB":
                    nc.tensor.matmul(work_bank[0:64, 0:D], vip_own[:, 0, :, :].rearrange("p h t -> p (h t)"),
                                     wout[:, 0, :], start=True, stop=True)
                    nc.tensor.matmul(work_bank[64:96, 0:D], vip_own[0:64, 2, 0:GH, :].rearrange("p h t -> p (h t)"),
                                     wout[0:64, 2, :], start=True, stop=True).then_inc(work_full, 1)
                elif kind == "TA":
                    pe.wait_ge(ip_step, b * 5 + 5)
                    for t in range(QT):
                        last_mm = nc.tensor.transpose(work_bank[:, t * 128:(t + 1) * 128], p_ip[:, t, 0:128], ident_f[:, :])
                    last_mm.then_inc(work_full, 1)
                elif kind == "TB":
                    for t in range(QT):
                        last_mm = nc.tensor.transpose(work_bank[0:96, t * 128:(t + 1) * 128], p_ip[:, t, 64:160], ident_f[:, :])
                    last_mm.then_inc(work_full, 1)

            def max_unit(group_no, g, u, first_group):
                h, t, half = u // (2 * QT), u // 2 % QT, u % 2
                if not (first_group and u < 2):
                    pe.wait_ge(max_taken, group_no * UNITS + u - 1)
                slot, q_slot = SLOTS[g % NG], g % NG
                for c in range(2):
                    keys = half * HALF + c * CHUNK
                    last = nc.tensor.matmul(max_bank[:, (u % 2) * 2 + c, 0:CHUNK],
                                            q_stack[0:STACK, q_slot, h, t * 128:(t + 1) * 128],
                                            k_stack[0:STACK, slot, h, keys:keys + CHUNK], start=True, stop=True)
                last.then_inc(max_scores, 1)

            def exp_tile(group_no, g, kt, j, first_group):
                n, slot = kt * GH + j, SLOTS[g]
                if not (first_group and n < 2):
                    pe.wait_ge(probs_ready, group_no * EXPS + n - 1)
                if kt < FULL:
                    last = nc.tensor.matmul(exp_bank[:, n % 2, :], k_stack[0:ROWS, slot, j, kt * 128:(kt + 1) * 128],
                                            q_stack[0:ROWS, g, j, :], start=True, stop=True)
                else:
                    for odd in range(2):
                        h = 2 * j + odd
                        last = nc.tensor.matmul(exp_bank[odd * TAIL:(odd + 1) * TAIL, n % 2, :],
                                                k_stack[0:ROWS, slot, h, FULL * 128:KEYS], q_stack[0:ROWS, g, h, :],
                                                start=True, stop=True)
                last.then_inc(scores_ready, 1)

            def pv_tile(group_no, g, kt):
                pe.wait_ge(probs_ready, group_no * EXPS + kt * GH + len(exps_of(kt)))
                if kt == 0:
                    pe.wait_ge(o_read, group_no)
                for h in range(GH):
                    head = g * GH + h
                    p = probs[:, kt % 2, h, :] if kt < FULL else probs_tail[:, h // 2, :]
                    last = nc.tensor.matmul(pv_bank[h * 32:h * 32 + VW, :], v_ones[:, kt, head * VW:(head + 1) * VW], p,
                                            start=(kt == 0), stop=(kt == FULL))
                last.then_inc(pv_done, 1)

            pe.wait_ge(weights_ip_loaded, 48)
            for g in range(NG):
                for half in range(2):
                    for ct in range(CT):
                        last = nc.tensor.matmul(work_bank[half * GR:(half + 1) * GR, g * 64:(g + 1) * 64],
                                                wk_ip[:, ct, g * GR:(g + 1) * GR], ctx_ip[:, ct, :],
                                                start=(ct == 0), stop=(ct == CT - 1))
            last.then_inc(work_full, 1)
            pe.wait_ge(work_empty, 1)
            for m, rows in enumerate((128, 128, 64)):
                for ct in range(CT):
                    last = nc.tensor.matmul(work_bank[0:rows, m * 64:(m + 1) * 64],
                                            wv_ip[:, ct, m * 128:m * 128 + rows], ctx_ip[:, ct, :],
                                            start=(ct == 0), stop=(ct == CT - 1))
            last.then_inc(work_full, 1)
            pe.wait_ge(weights_loaded, 112)
            pe.wait_ge(ctx_loaded, CT * 16)
            pe.wait_ge(x_loaded, 32)
            pe.wait_ge(consts_loaded, 80)
            for g in range(2):
                for c in range(2):
                    pe.wait_ge(work_empty, PRO_ORDER["K", g, c])
                    k_piece(g, c, TURNS[2])
                pe.wait_ge(work_empty, PRO_ORDER["Q", g])
                q_piece(g)
                ip_piece(g, PRO_ORDER["Q", g], 1)
            units = iter(range(UNITS))
            pe.wait_ge(stack_loaded[0], 96)
            for t in range(V_EARLY):
                pe.wait_ge(work_empty, PRO_ORDER["V", t])
                v_piece(t, TURNS[2])
                for _ in range(6):
                    u = next(units, None)
                    if u is not None:
                        max_unit(0, 0, u, True)
            pe.wait_ge(cleared, 8)
            pe.wait_ge(work_empty, PRO_ORDER["NEG", 0])
            negative_piece(0)
            pe.wait_ge(ones_ready, 1)

            def body(b, first, last):
                plan = work_plan(first, last)
                for g in range(NG):
                    group_no = b * NG + g
                    units = iter(range(UNITS))

                    def next_units(n):
                        for _ in range(n):
                            u = next(units)
                            if u == 0:
                                nb = b + 1 if g < NG - 1 else b + 2
                                pe.wait_ge(stack_loaded[(g + 1) % NG], nb * 96)
                            max_unit(group_no + 1, g + 1, u, False)

                    pe.wait_ge(neg_loaded, (group_no + 1) * 16)
                    for kt in range(KT):
                        places = (0,) * 4 if last and g == NG - 1 else units_at(g, kt)
                        exp_tile(group_no, g, kt, 0, first and g == 0)
                        next_units(places[0])
                        exp_tile(group_no, g, kt, 1, first and g == 0)
                        if kt == NEG_AT and not (last and g == NG - 1):
                            pe.wait_ge(work_empty, work_number(b, ("NEG", g + 1), first, last))
                            negative_piece(group_no + 1)
                        made_late = kt - 1 if g == 0 else FULL if (g, kt) == (1, 0) else 0
                        if made_late >= V_EARLY:
                            pe.wait_ge(work_empty, work_number(b, ("V", made_late), first, last) + 1)
                        if kt:
                            pv_tile(group_no, g, kt - 1)
                        elif g or not first:
                            pv_tile(group_no - 1, (g - 1) % NG, FULL)
                        next_units(places[1])
                        if kt < FULL:
                            exp_tile(group_no, g, kt, 2, first and g == 0)
                            next_units(places[2])
                            exp_tile(group_no, g, kt, 3, first and g == 0)
                        if (g, kt) in plan:
                            work(b, *plan[g, kt], first, last)
                        next_units(places[3])

            batches(pe, body)
            pv_tile(B * NG - 1, NG - 1, FULL)
            end = len(PRO) + FIRST_WORK + (B - 2) * LOOP_WORK + len(work_order(False, True))
            pe.wait_ge(o_packed, B * NG * 64)
            for t in range(QT):
                pe.wait_ge(work_empty, end + t)
                out_piece(t, TURNS[2])

        @block.scalar
        def _(act):
            def copy(dst, src):
                return nc.scalar.activation(dst, src, ACT.Copy)

            def k_first_part(b, g, c, number):
                act.wait_ge(work_full, number + 1)
                if c == 0:
                    act.wait_ge(k_stored, (b * NG + g) * 32)
                copy(k_parts[:, 0, c * CHUNK:(c + 1) * CHUNK], work_bank[:, 0:CHUNK]).then_inc(k_high, 1)

            def q_copy(b, g, number):
                act.wait_ge(work_full, number + 1)
                act.wait_ge(q_step, (b * NG + g) * 4)
                copy(q_full[:, :], work_bank[:, 0:QHALF]).then_inc(work_empty, 1)

            def v_copy(b, t, number, reused):
                act.wait_ge(work_full, number + 1)
                if reused:
                    act.wait_ge(pv_done, (b * NG - 1) * KT + t + 1)
                v = v_ones[:, t, :].rearrange("p (h d) -> p h d", d=VW)
                w = work_bank[:, 0:D].rearrange("p (h d) -> p h d", d=DH)
                if t < FULL:
                    copy(v[:, :, 0:DH], w[:, :, :]).then_inc(work_empty, 1)
                else:
                    copy(v[0:TAILV, 0:HEADS:2, 0:DH], w[0:TAILV, 0:HEADS:2, :])
                    copy(v[TAIL:TAIL + TAILV, 1:HEADS:2, 0:DH], w[TAIL:TAIL + TAILV, 1:HEADS:2, :]).then_inc(work_empty, 1)

            def negative_copy(group_no, g, number, first_group):
                act.wait_ge(work_full, number + 1)
                if not first_group:
                    act.wait_ge(neg_loaded, group_no * 16)
                copy(neg_rows[:, :], work_bank[:, :].bitcast(BF16)[0:PARTS * UNITS // 2, 0:128]).then_inc(work_empty, 1)
                act.wait_ge(work_empty, number + 1)
                act.dma_start(q_stack[STACK:ROWS, g % NG, :, :], neg_rows[:, :]).then_inc(neg_loaded, 16)

            def exp_tile(group_no, kt, j, first_group):
                n = kt * GH + j
                act.wait_ge(scores_ready, group_no * EXPS + n + 1)
                if j == 0:
                    if kt == FULL:
                        if not first_group:
                            act.wait_ge(pv_done, group_no * KT)
                    elif kt >= 2:
                        act.wait_ge(pv_done, group_no * KT + kt - 1)
                    elif not first_group:
                        act.wait_ge(pv_done, group_no * KT + kt - 2)
                dst = probs[:, kt % 2, j, :] if kt < FULL else probs_tail[:, j, :]
                nc.scalar.activation(dst, exp_bank[:, n % 2, :], ACT.Exp, scale=SCALE).then_inc(probs_ready, 1)

            def o_copy(group_no):
                act.wait_ge(pv_done, (group_no + 1) * KT)
                act.wait_ge(o_packed, group_no * 64)
                copy(o_sum[:, :], pv_bank[:, :]).then_inc(o_read, 1)

            act.wait_ge(work_full, 1)
            copy(kip[:, :, :].rearrange("p g n -> p (g n)"), work_bank[:, 0:D]).then_inc(work_empty, 1)
            act.wait_ge(work_full, 2)
            copy(vip[:, 0:2, :].rearrange("p m n -> p (m n)"), work_bank[:, 0:128])
            copy(vip[0:64, 2, :], work_bank[0:64, 128:192]).then_inc(work_empty, 1)
            for g in range(2):
                for c in range(2):
                    k_first_part(0, g, c, PRO_ORDER["K", g, c])
                q_copy(0, g, PRO_ORDER["Q", g])
            act.wait_ge(cleared, 8)
            for t in range(V_EARLY):
                v_copy(0, t, PRO_ORDER["V", t], False)
            negative_copy(0, 0, PRO_ORDER["NEG", 0], True)

            def body(b, first, last):
                plan = work_plan(first, last)
                for g in range(NG):
                    group_no = b * NG + g
                    for kt in range(KT):
                        tiles = list(exps_of(kt))
                        for j in tiles[:2]:
                            exp_tile(group_no, kt, j, first and g == 0)
                        if kt == 0 and (g or not first):
                            o_copy(group_no - 1)
                        if kt == NEG_AT and not (last and g == NG - 1):
                            negative_copy(group_no + 1, g + 1, work_number(b, ("NEG", g + 1), first, last), False)
                        for j in tiles[2:]:
                            exp_tile(group_no, kt, j, first and g == 0)
                        if (g, kt) == (3, 0):
                            act.wait_ge(ip_step, b * 5 + 3)
                            nc.scalar.activation(s_ip[:, :, :], s_ip[:, :, :], ACT.Exp).then_inc(ip_exp, 1)
                        piece, turn = plan.get((g, kt), (None, 0))
                        if turn == 0:
                            continue
                        kind, number = piece[0], work_number(b, piece, first, last)
                        if kind == "K":
                            k_first_part(b, piece[1], piece[2], number)
                        elif kind == "Q":
                            q_copy(b, piece[1], number)
                        elif kind == "V":
                            if piece[1] >= V_EARLY:
                                v_copy(b, piece[1], number, not first)
                            else:
                                v_copy(b + 1, piece[1], number, True)
                        elif kind == "WA":
                            act.wait_ge(work_full, number + 1)
                            copy(wout[64:128, 3, :], work_bank[64:128, 0:D]).then_inc(work_empty, 1)
                        elif kind == "WB":
                            act.wait_ge(work_full, number + 1)
                            copy(wout[0:64, 3, :], work_bank[0:64, 0:D])
                            copy(wout[64:96, 2, :], work_bank[64:96, 0:D]).then_inc(work_empty, 1)
                        elif kind == "TA":
                            act.wait_ge(work_full, number + 1)
                            copy(o_t[:, 3, :], work_bank[:, :]).then_inc(work_empty, 1)
                        elif kind == "TB":
                            act.wait_ge(work_full, number + 1)
                            copy(o_t[64:96, 2, :], work_bank[64:96, :]).then_inc(work_empty, 1)

            batches(act, body)
            o_copy(B * NG - 1)

        @block.vector
        def _(dve):
            def k_remainder(b, g, c, number, reused=True):
                dve.wait_ge(k_high, (b * NG + g) * 2 + c + 1)
                if reused:
                    dve.wait_ge(k_split, (b * NG + g) * 2 + c - 1)
                nc.vector.tensor_tensor(k_rest[:, c, :], work_bank[:, 0:CHUNK], k_parts[:, 0, c * CHUNK:(c + 1) * CHUNK],
                                        ALU.subtract).then_inc(work_empty, 1)

            def ip_scale(g, number):
                dve.wait_ge(work_full, number + 1)
                src = work_bank[:, 0:128].rearrange("p (n f m) -> p n f m", n=2, f=2)
                for half in range(2):
                    last = nc.vector.tensor_scalar(
                        s_ip[:, half * 2:half * 2 + 2, (g % NG) * 32:(g % NG + 1) * 32], src[:, :, half, :], SCALE, None, ALU.mult)
                last.then_inc(work_empty, 1)

            def take_max(group_no, u):
                dve.wait_ge(max_scores, group_no * UNITS + u + 1)
                nc.vector.reduce_max(half_max[:, u:u + 1], max_bank[:, (u % 2) * 2:(u % 2) * 2 + 2, 0:CHUNK], AX.XY)\
                  .then_inc(max_taken, 1)

            def negative_parts(group_no):
                dve.wait_ge(max_taken, (group_no + 1) * UNITS)
                nc.vector.reduce_max(neg_max[:, :], half_max[:, :].rearrange("p (m f) -> p m f", f=2), AX.X, negate=True)\
                  .then_inc(neg_step, 1)
                dve.wait_ge(neg_step, group_no * 5 + 1)
                nc.vector.tensor_copy(neg_parts[:, 0, :], neg_max[:, :]).then_inc(neg_step, 1)
                dve.wait_ge(neg_step, group_no * 5 + 2)
                nc.vector.tensor_tensor(neg_rest[:, :], neg_max[:, :], neg_parts[:, 0, :], ALU.subtract).then_inc(neg_step, 1)
                dve.wait_ge(neg_step, group_no * 5 + 3)
                nc.vector.tensor_copy(neg_parts[:, 1, :], neg_rest[:, :]).then_inc(neg_step, 1)
                dve.wait_ge(neg_step, group_no * 5 + 4)
                nc.vector.tensor_tensor(neg_parts[:, 2, :], neg_rest[:, :], neg_parts[:, 1, :], ALU.subtract)\
                  .then_inc(neg_step, 1)

            def invert_sums(group_no):
                dve.wait_ge(sums_loaded, (group_no + 1) * 16)
                dve.wait_ge(recips_stored, group_no * 16)
                nc.vector.reciprocal(recips[:, :], sums[:, :]).then_inc(recips_ready, 1)

            def ip_softmax_1(b, number):
                scores = s_ip[:, :, :].rearrange("p q (h t) -> p q h t", t=IPT)
                m = mask[:, bass.ds(b, 1), :, :].rearrange("p o q t -> p (o q) t")
                dve.wait_ge(work_empty, number + 1)
                nc.vector.tensor_tensor(scores, scores, m.unsqueeze(2).to_broadcast([128, QT, HEADS, IPT]), ALU.add)\
                  .then_inc(ip_step, 1)
                dve.wait_ge(ip_step, b * 5 + 1)
                nc.vector.reduce_max(ip_max[:, :, :], scores, AX.X).then_inc(ip_step, 1)
                dve.wait_ge(ip_step, b * 5 + 2)
                nc.vector.tensor_tensor(scores, scores, ip_max[:, :, :].unsqueeze(3).to_broadcast([128, QT, HEADS, IPT]),
                                        ALU.subtract).then_inc(ip_step, 1)

            def ip_softmax_2(b):
                scores = s_ip[:, :, :].rearrange("p q (h t) -> p q h t", t=IPT)
                dve.wait_ge(ip_exp, b + 1)
                nc.vector.reduce_sum(ip_sum[:, :, :], scores, AX.X).then_inc(ip_exp_sum, 1)
                dve.wait_ge(ip_exp_sum, b + 1)
                nc.vector.reciprocal(ip_max[:, :, :], ip_sum[:, :, :]).then_inc(ip_step, 1)
                dve.wait_ge(ip_step, b * 5 + 4)
                nc.vector.tensor_tensor(p_ip[:, :, :].rearrange("p q (h t) -> p q h t", t=IPT), scores,
                                        ip_max[:, :, :].unsqueeze(3).to_broadcast([128, QT, HEADS, IPT]), ALU.mult)\
                  .then_inc(ip_step, 1)

            def out_add(b, t, number):
                dve.wait_ge(work_full, number + 1)
                if t == 0:
                    dve.wait_ge(residual_loaded, b * 16)
                dve.wait_ge(out_stored[t % 2], ((b - 1) * 2 + t // 2) * 16)
                nc.vector.tensor_tensor(out_sb[:, t % 2, :], work_bank[:, 0:D], xres[:, t, :], ALU.add)\
                  .then_inc(work_empty, 1)

            nc.vector.memset(pv_bank[:, :], 0.0).then_inc(cleared, 1)
            nc.vector.memset(v_ones[:, :, :], 0.0).then_inc(mask_step, 1)
            dve.wait_ge(mask_step, 1)
            v = v_ones[:, :, :].rearrange("p t (h d) -> p t h d", d=VW)
            nc.vector.memset(v[:, 0:FULL, :, DH], 1.0).then_inc(cleared, 1)
            nc.vector.memset(v[0:TAILV, FULL, 0:HEADS:2, DH], 1.0).then_inc(cleared, 1)
            nc.vector.memset(v[TAIL:TAIL + TAILV, FULL, 1:HEADS:2, DH], 1.0).then_inc(cleared, 1)
            nc.vector.memset(o_t[96:97, 2, :], 1.0).then_inc(cleared, 1)

            dve.wait_ge(consts_loaded, 80)
            nc.vector.tensor_copy(ident_b[:, :], ident_f[:, :]).then_inc(cleared, 1)

            nc.vector.memset(neg_parts[:, :, :], 0.0).then_inc(cleared, 1)
            nc.vector.memset(zero[:, :], 0.0).then_inc(cleared, 1)

            tests = ((0, 0, ALU.is_ge), (1, 1, ALU.is_ge), (0, 2, ALU.is_le), (1, 3, ALU.is_le))
            step = 1
            for n, (axis, corner, op) in enumerate(tests):
                place = grid_sb[:, axis, :].unsqueeze(1).unsqueeze(3).to_broadcast([128, B, QT, 4])
                limit = box[:, :, :, corner].unsqueeze(2).to_broadcast([128, B, QT, 4])
                nc.vector.tensor_tensor((cmp if n else inside)[:, :, :, :], place, limit, op).then_inc(mask_step, 1)
                step += 1
                dve.wait_ge(mask_step, step)
                if n:
                    nc.vector.tensor_tensor(inside[:, :, :, :], inside[:, :, :, :], cmp[:, :, :, :], ALU.mult)\
                      .then_inc(mask_step, 1)
                    step += 1
                    dve.wait_ge(mask_step, step)
            nc.vector.tensor_scalar(mask[:, :, :, IPT // 2:IPT], inside[:, :, :, :], -NEG, NEG, ALU.mult, ALU.add)\
              .then_inc(mask_step, 1)
            nc.vector.reduce_max(outside[:, :, :], inside[:, :, :, :], AX.X).then_inc(mask_step, 1)
            dve.wait_ge(mask_step, step + 2)
            nc.vector.tensor_scalar(mask[:, :, :, 0:IPT // 2], outside[:, :, :].unsqueeze(3).to_broadcast([128, B, QT, 4]),
                                    NEG, None, ALU.mult).then_inc(mask_step, 1)
            dve.wait_ge(mask_step, step + 3)

            for g in range(2):
                for c in range(2):
                    k_remainder(0, g, c, PRO_ORDER["K", g, c], g > 0)
                ip_scale(g, PRO_ORDER["IP", g])
            for u in range(UNITS):
                take_max(0, u)
            negative_parts(0)

            def body(b, first, last):
                plan = work_plan(first, last)
                for g in range(NG):
                    group_no = b * NG + g
                    units = iter(range(UNITS))
                    for kt in range(KT):
                        places = (0,) * 4 if last and g == NG - 1 else units_at(g, kt)
                        for _ in range(sum(places)):
                            u = next(units)
                            take_max(group_no + 1, u)
                            if u == UNITS - 1:
                                negative_parts(group_no + 1)
                        piece, turn = plan.get((g, kt), (None, 0))
                        if kt == INVERT_AT[g] and (g or not first):
                            invert_sums(group_no - 1)
                        if turn != 0:
                            number = work_number(b, piece, first, last)
                            if piece[0] == "K":
                                k_remainder(b, piece[1], piece[2], number)
                            elif piece[0] == "IP":
                                ip_scale(piece[1], number)
                            elif piece[0] == "OUT":
                                out_add(b, piece[1], number)
                        if (g, kt) == (3, 0):
                            ip_softmax_1(b, work_number(b, ("IP", 4), first, last))
                        if (g, kt) == (3, 1):
                            ip_softmax_2(b)

            batches(dve, body)
            end = len(PRO) + FIRST_WORK + (B - 2) * LOOP_WORK + len(work_order(False, True))
            invert_sums(B * NG - 1)
            for t in range(QT):
                out_add(B, t, end + t)

        @block.gpsimd
        def _(pool):
            def split_k(b, g, c, number):
                pool.wait_ge(work_empty, number + 1)
                part = k_parts[:, :, c * CHUNK:(c + 1) * CHUNK]
                nc.gpsimd.tensor_tensor(part[:, 1, :], k_rest[:, c, :], zero[:, :].to_broadcast([128, CHUNK]), ALU.add).then_inc(k_mid, 1)
                pool.wait_ge(k_mid, (b * NG + g) * 2 + c + 1)
                nc.gpsimd.tensor_tensor(part[:, 2, :], k_rest[:, c, :], part[:, 1, :], ALU.subtract).then_inc(k_split, 1)

            def split_q(b, g, number):
                done = (b * NG + g) * 4
                pool.wait_ge(work_empty, number + 1)
                pool.wait_ge(q_stored, (b * NG + g) * 32)
                nc.gpsimd.tensor_tensor(q_parts[:, 0, :], q_full[:, :], zero[:, :].to_broadcast([128, QHALF]), ALU.add).then_inc(q_step, 1)
                pool.wait_ge(q_step, done + 1)
                nc.gpsimd.tensor_tensor(q_rest[:, :], q_full[:, :], q_parts[:, 0, :], ALU.subtract).then_inc(q_step, 1)
                pool.wait_ge(q_step, done + 2)
                nc.gpsimd.tensor_tensor(q_parts[:, 1, :], q_rest[:, :], zero[:, :].to_broadcast([128, QHALF]), ALU.add).then_inc(q_step, 1)
                pool.wait_ge(q_step, done + 3)
                nc.gpsimd.tensor_tensor(q_parts[:, 2, :], q_rest[:, :], q_parts[:, 1, :], ALU.subtract).then_inc(q_step, 1)

            def own_k(b):
                src = kip[:, :, bass.ds(b * IPT, IPT)].unsqueeze(2).to_broadcast([128, NG, 8, IPT])
                nc.gpsimd.tensor_tensor(kip_own[:, :, :, :], src,
                                        own_k_sb[:, :].unsqueeze(1).unsqueeze(3).to_broadcast([128, NG, 8, IPT]), ALU.mult)\
                  .then_inc(kip_ready, 1)

            def own_v(b):
                src = vip[:, :, bass.ds(b * IPT, IPT)]
                nc.gpsimd.tensor_tensor(vip_own[:, 0:2, :, :], src[:, 0:2, :].unsqueeze(2).to_broadcast([128, 2, 8, IPT]),
                                        own_v_sb[:, :].unsqueeze(1).unsqueeze(3).to_broadcast([128, 2, 8, IPT]), ALU.mult)
                nc.gpsimd.tensor_tensor(vip_own[0:64, 2, 0:GH, :], src[0:64, 2, :].unsqueeze(1).to_broadcast([64, GH, IPT]),
                                        own_v_sb[0:64, 0:GH].unsqueeze(2).to_broadcast([64, GH, IPT]), ALU.mult).then_inc(vip_ready, 1)

            def scale_o(group_no):
                pool.wait_ge(r_wide_loaded, (group_no + 1) * 16)
                nc.gpsimd.tensor_tensor(o_sum[:, :], o_sum[:, :], r_wide[:, :], ALU.mult).then_inc(o_scaled, 1)

            pool.dma_start(own_k_sb[:, :], own_k_rows).then_inc(consts_loaded, 16)
            pool.dma_start(own_v_sb[:, :], own_v_rows).then_inc(consts_loaded, 16)
            pool.dma_start(ident_f[:, :], ident).then_inc(consts_loaded, 16)
            pool.dma_start(grid_sb[:, :, :], grid).then_inc(consts_loaded, 16)
            pool.dma_start(box[:, :, :, :].rearrange("p b m k -> p (b m k)"),
                           boxes.rearrange("b m k -> (b m k)").partition_broadcast(128)).then_inc(consts_loaded, 16)
            pool.wait_ge(consts_loaded, 80)
            pool.wait_ge(cleared, 8)
            pool.wait_ge(work_empty, 2)
            own_k(0)
            for g in range(2):
                for c in range(2):
                    split_k(0, g, c, PRO_ORDER["K", g, c])
                split_q(0, g, PRO_ORDER["Q", g])
            pool.wait_ge(q_step, 8)
            nc.gpsimd.memset(k_stack[STACK:ROWS, :, :, :], 1.0).then_inc(ones_ready, 1)
            pool.wait_ge(ones_ready, 1)

            def body(b, first, last):
                number = lambda piece: work_number(b, piece, first, last)
                for g in range(NG):
                    splits = [p for p in SPLITS[g] if not (last and p[1] > 4)]
                    for n, piece in enumerate(splits):
                        if n == SCALE_AT[g] and (g or not first):
                            scale_o(b * NG + g - 1)
                        if piece[0] == "K":
                            split_k(b, piece[1], piece[2], number(piece))
                        else:
                            split_q(b, piece[1], number(piece))
                    if len(splits) <= SCALE_AT[g]:
                        scale_o(b * NG + g - 1)
                    if g == 1:
                        own_v(b)
                    if g == 2 and not last:
                        pool.wait_ge(work_full, number(("IP", 4)) + 1)
                        own_k(b + 1)

            batches(pool, body)
            scale_o(B * NG - 1)


def kernel(x, ctx_2048, fside_Bx4x4_0, L0_xattn_w_q, L0_xattn_w_k, L0_xattn_w_v, L0_xattn_w_k_ip, L0_xattn_w_v_ip,
           L0_xattn_w_out, L0_xattn_b_out):
    import concourse.bacc as bacc
    from concourse.bass_utils import run_bass_kernel_spmd

    x, ctx = np.asarray(x), np.asarray(ctx_2048)
    text = np.concatenate([ctx[:, :TEXT], ctx[:, :KEYS - TEXT]], axis=1)
    q = np.arange(S)
    step_x = (np.arange(GRID_W, dtype=np.float32) / np.float32(GRID_W - 1)).astype(np.float32)
    step_y = (np.arange(GRID_H, dtype=np.float32) / np.float32(GRID_H - 1)).astype(np.float32)
    places = np.stack([step_x[q % GRID_W], step_y[q // GRID_W]])
    rows = np.arange(128)[:, None]

    def dims_first(w):
        w = np.asarray(w)
        return w.reshape(-1, NG, GH, DH).transpose(0, 1, 3, 2).reshape(w.shape)

    arrays = {
        "x": x,
        "x_t": x.transpose(0, 2, 1),
        "ctx_t": text.transpose(0, 2, 1),
        "ctx_ip_t": ctx[:, TEXT:].transpose(2, 0, 1).reshape(C, B * IPT),
        "boxes": np.asarray(fside_Bx4x4_0),
        "grid": places.reshape(2, QT, 128).transpose(2, 0, 1),
        "own_k_rows": (rows // GR * GH + rows % GH == np.arange(8)[None, :]).astype(np.float32),
        "own_v_rows": (rows // DH == np.arange(8)[None, :]).astype(np.float32),
        "ident": np.eye(128, dtype=np.float32),
        "w_q": dims_first(L0_xattn_w_q), "w_k": dims_first(L0_xattn_w_k), "w_v": L0_xattn_w_v,
        "w_k_ip": dims_first(L0_xattn_w_k_ip),
        "w_v_ip": L0_xattn_w_v_ip, "w_out": L0_xattn_w_out, "b_out": L0_xattn_b_out,
    }
    nc = bacc.Bacc("TRN2", target_bir_lowering=False, num_devices=1)
    feeds, args = {}, []
    for name, a in arrays.items():
        a = np.ascontiguousarray(a)
        feeds[f"in_{name}"] = a
        args.append(nc.dram_tensor(f"in_{name}", a.shape, mybir.dt.from_np(a.dtype), kind="ExternalInput").ap())
    out = nc.dram_tensor("out", (B, S, D), FP32, kind="ExternalOutput").ap()
    cross_attention(nc, *args, out)
    r = run_bass_kernel_spmd(nc, [feeds], core_ids=[0])
    return r.results[0]["out"]
```

```python
import numpy as np
import concourse.bass as bass
from concourse import mybir
from contextlib import ExitStack

FP32 = mybir.dt.float32
BF16 = mybir.dt.bfloat16
ALU = mybir.AluOpType
ACT = mybir.ActivationFunctionType
AX = mybir.AxisListType

B, S, D, C = 8, 512, 320, 512
HEADS, DH = 20, 16
TOKENS = 1601
IPT = 8
TEXT = TOKENS - IPT
KEYS = 1600
GH = 4
NG = HEADS // GH
GR = GH * DH
CT = C // 128
QT = S // 128
FULL = KEYS // 128
TAIL = KEYS - FULL * 128
TAILV = TEXT - FULL * 128
KT = FULL + 1
HALF = KEYS // 2
CHUNK = HALF // 2
QHALF = S // 2
VW = DH + 1
PARTS = 3
RUNS = ((0, 3), (3, 2), (5, 1))
STACK = 6 * DH
ROWS = STACK + PARTS
SLOTS = (0, 1, 2, 3, 2)
EXPS = FULL * GH + GH // 2
UNITS = GH * QT * 2
SCALE = float(DH) ** -0.5
NEG = -10000.0
GRID_W, GRID_H = 32, 16
V_EARLY = 6


def share(steps, turn):
    n, m = turn
    return range(steps * n // m, steps * (n + 1) // m)


WHOLE = (0, 1)


def work_plan(first, last):
    turns = {("Q", 2): (0, 0), ("K", 2, 0): (0, 1, 2), ("K", 2, 1): (0, 3, 4), ("IP", 2): (0, 5),
             ("K", 3, 0): (1, 0, 1), ("K", 3, 1): (1, 2, 3), ("Q", 3): (1, 4), ("IP", 3): (1, 5), ("K", 4, 0): (1, 12),
             ("K", 4, 1): (2, 0, 1, 2, 3), ("Q", 4): (2, 4, 5, 6), ("IP", 4): (2, 7), ("WA",): (2, 9), ("WB",): (2, 10, 11),
             ("TA",): (3, 10), ("TB",): (3, 11)}
    turns.update({("V", t): (0, t) for t in range(V_EARLY, KT)})
    if not first:
        turns.update({("OUT", 0): (1, 6, 7), ("OUT", 1): (1, 8, 9), ("OUT", 2): (1, 10), ("OUT", 3): (1, 11)})
    if not last:
        turns.update({("K", 5, 0): (2, 12), ("K", 5, 1): (3, 0, 1, 2, 3), ("Q", 5): (3, 4), ("IP", 5): (3, 5),
                      ("Q", 6): (3, 6, 7, 8), ("IP", 6): (3, 9), ("K", 6, 0): (3, 12), ("K", 6, 1): (4, 0, 1)})
        turns.update({("V", t): (4, 2 * t + 2, 2 * t + 3) for t in range(V_EARLY - 1)})
        turns["V", V_EARLY - 1] = (4, KT - 1)
    else:
        turns.update({("WB",): (2, 12), ("TA",): (3, 11), ("TB",): (3, 12)})
    plan = {}
    for piece, (g, *kts) in turns.items():
        for n, kt in enumerate(kts):
            assert (g, kt) not in plan
            plan[g, kt] = (piece, (n, len(kts)))
    return plan


def begins(turn):
    return turn is not None and turn[0] == 0


def ends(turn):
    return turn is not None and turn[0] == turn[1] - 1


SPLITS = ((("Q", 2), ("K", 2, 0), ("K", 2, 1)), (("K", 3, 0), ("K", 3, 1), ("Q", 3)),
          (("K", 4, 0), ("K", 4, 1), ("Q", 4)), (("K", 5, 0), ("K", 5, 1), ("Q", 5), ("Q", 6)), (("K", 6, 0), ("K", 6, 1)))
SCALE_AT = (0, 3, 1, 2, 2)
NEG_AT = FULL
INVERT_AT = (2, 2, 2, 3, 2)


def work_order(first, last):
    plan, order = work_plan(first, last), {}
    for g in range(NG):
        for kt in range(KT):
            if kt == NEG_AT and not (last and g == NG - 1):
                order["NEG", g + 1] = len(order)
            piece, turn = plan.get((g, kt), (None, None))
            if begins(turn):
                order[piece] = len(order)
    return order


PRO_PLAN = [(p, WHOLE, 0) for p in (("K", 0, 0), ("K", 0, 1), ("Q", 0), ("KIP",), ("IP", 0), ("K", 1, 0))]
PRO_PLAN += [(("K", 1, 1), (0, 2), 2), (("K", 1, 1), (1, 2), 2), (("Q", 1), WHOLE, 2), (("IP", 1), WHOLE, 1)]
PRO_PLAN += [(("VIP",), WHOLE, 2)]
PRO_PLAN += [(("V", t), (n, 2), 3 if 2 * t + n in (1, 5, 8) else 2) for t in range(V_EARLY - 1) for n in range(2)]
PRO_PLAN += [(("NEG", 0), WHOLE, 0), (("V", V_EARLY - 1), WHOLE, 0)]
assert sum(n for _, _, n in PRO_PLAN) == UNITS
PRO = [piece for piece, turn, _ in PRO_PLAN if begins(turn)]
PRO_ORDER = {p: n for n, p in enumerate(PRO)}
FIRST_WORK = len(work_order(True, False))
LOOP_WORK = len(work_order(False, False))


UNITS_AT = ((3, 3, 3, 3, 3, 3, 3, 3, 3, 2, 2, 1), (3, 3, 3, 3, 3, 3, 3, 3, 3, 2, 2, 1),
            (3, 3, 3, 3, 3, 3, 3, 3, 2, 2, 3, 1), (0, 0, 4, 4, 4, 3, 3, 4, 3, 3, 3, 1), (3, 3, 3, 3, 3, 3, 3, 3, 3, 2, 2, 1))
PLACES = ((0, 0, 0, 0), (1, 0, 0, 0), (1, 0, 1, 0), (1, 1, 1, 0), (1, 1, 1, 1), (1, 1, 1, 2))
LAST_PLACES = ((0, 0, 0, 0), (1, 0, 0, 0), (1, 1, 0, 0), (1, 1, 1, 0), (1, 1, 1, 1))
assert all(sum(u) == UNITS for u in UNITS_AT)


def units_at(g, kt):
    if kt >= len(UNITS_AT[g]):
        return PLACES[0]
    return (LAST_PLACES if kt == len(UNITS_AT[g]) - 1 else PLACES)[UNITS_AT[g][kt]]


def exps_of(kt):
    return range(GH) if kt < FULL else range(GH // 2)


def cross_attention(nc, x, x_t, ctx_t, ctx_ip_t, boxes, grid, own_k_rows, own_v_rows, ident, w_q, w_k, w_v, w_k_ip, w_v_ip,
                    w_out, b_out, out):
    scratch_k = nc.dram_tensor("scratch_k", (NG, PARTS, GR, KEYS), BF16, kind="Internal").ap()
    scratch_q = nc.dram_tensor("scratch_q", (NG, PARTS, GR, S), BF16, kind="Internal").ap()
    scratch_r = nc.dram_tensor("scratch_r", (GH, S), FP32, kind="Internal").ap()

    ctx = ExitStack()
    with ctx:
        def sb(name, shape, dt=FP32):
            return ctx.enter_context(nc.sbuf_tensor(name, shape, dt))

        def sem(name):
            return ctx.enter_context(nc.semaphore(name))

        wq = sb("wq", [128, 3, D])
        wk = sb("wk", [128, CT, D])
        wv = sb("wv", [128, CT, D])
        wout = sb("wout", [128, 4, D])
        own_k_sb = sb("own_k_sb", [128, 8])
        own_v_sb = sb("own_v_sb", [128, 8])
        ident_f = sb("ident_f", [128, 128])
        ident_b = sb("ident_b", [128, 128], BF16)
        grid_sb = sb("grid_sb", [128, 2, QT])
        box = sb("box", [128, B, 4, 4])
        inside = sb("inside", [128, B, QT, 4])
        cmp = sb("cmp", [128, B, QT, 4])
        outside = sb("outside", [128, B, QT])
        mask = sb("mask", [128, B, QT, IPT])
        ctxt = sb("ctxt", [128, CT, KEYS])
        xt = sb("xt", [128, 3, S])
        xres = sb("xres", [128, QT, D])
        k_parts = sb("k_parts", [128, PARTS, HALF], BF16)
        k_rest = sb("k_rest", [128, 2, CHUNK])
        q_full = sb("q_full", [128, QHALF])
        q_rest = sb("q_rest", [128, QHALF])
        q_parts = sb("q_parts", [128, PARTS, QHALF], BF16)
        k_stack = sb("k_stack", [128, 4, GH, KEYS], BF16)
        q_stack = sb("q_stack", [128, NG, GH, S], BF16)
        v_ones = sb("v_ones", [128, KT, HEADS * VW])
        probs = sb("probs", [128, 2, GH, S])
        probs_tail = sb("probs_tail", [128, GH // 2, S])
        half_max = sb("half_max", [128, UNITS])
        neg_max = sb("neg_max", [128, UNITS // 2])
        neg_rest = sb("neg_rest", [128, UNITS // 2])
        neg_parts = sb("neg_parts", [128, 8, UNITS // 2], BF16)
        neg_rows = sb("neg_rows", [PARTS * UNITS // 2, 128], BF16)
        zero = sb("zero", [128, 1])
        o_sum = sb("o_sum", [128, S])
        sums = sb("sums", [128, GH * S // 128])
        recips = sb("recips", [128, GH * S // 128])
        r_wide = sb("r_wide", [128, S])
        o_t = sb("o_t", [128, 4, S])
        kip = sb("kip", [128, NG, B * IPT])
        vip = sb("vip", [128, 3, B * IPT])
        kip_own = sb("kip_own", [128, NG, 8, IPT])
        vip_own = sb("vip_own", [128, 3, 8, IPT])
        s_ip = sb("s_ip", [128, QT, HEADS * IPT])
        p_ip = sb("p_ip", [128, QT, HEADS * IPT])
        ip_max = sb("ip_max", [128, QT, HEADS])
        ip_sum = sb("ip_sum", [128, QT, HEADS])
        early = probs[:, :, :, :].rearrange("p a h n -> p (a h n)")
        wk_ip = early[:, 0:CT * D].rearrange("p (c n) -> p c n", c=CT)
        wv_ip = early[:, CT * D:2 * CT * D].rearrange("p (c n) -> p c n", c=CT)
        ctx_ip = early[:, 2 * CT * D:2 * CT * D + CT * B * IPT].rearrange("p (c n) -> p c n", c=CT)

        exp_bank = ctx.enter_context(nc.psum_tensor("exp_bank", [128, 2, 512], FP32))
        max_bank = ctx.enter_context(nc.psum_tensor("max_bank", [128, 4, 512], FP32))
        pv_bank = ctx.enter_context(nc.psum_tensor("pv_bank", [128, 512], FP32))
        work_bank = ctx.enter_context(nc.psum_tensor("work_bank", [128, 512], FP32))

        weights_ip_loaded = sem("weights_ip_loaded")
        wk_loaded = sem("wk_loaded")
        wq_loaded = sem("wq_loaded")
        weights_loaded = sem("weights_loaded")
        consts_loaded = sem("consts_loaded")
        ctx_first_loaded = sem("ctx_first_loaded")
        ctx_loaded = sem("ctx_loaded")
        x_loaded = sem("x_loaded")
        residual_loaded = sem("residual_loaded")
        cleared = sem("cleared")
        mask_step = sem("mask_step")
        k_high = sem("k_high")
        k_mid = sem("k_mid")
        k_split = sem("k_split")
        k_stored = sem("k_stored")
        q_step = sem("q_step")
        q_stored = sem("q_stored")
        stack_loaded = [sem(f"stack_loaded{g}") for g in range(NG)]
        scores_ready = sem("scores_ready")
        probs_ready = sem("probs_ready")
        pv_done = sem("pv_done")
        max_scores = sem("max_scores")
        max_taken = sem("max_taken")
        neg_step = sem("neg_step")
        neg_loaded = sem("neg_loaded")
        o_read = sem("o_read")
        sums_loaded = sem("sums_loaded")
        recips_ready = sem("recips_ready")
        recips_stored = sem("recips_stored")
        r_wide_loaded = sem("r_wide_loaded")
        o_scaled = sem("o_scaled")
        o_packed = sem("o_packed")
        kip_ready = sem("kip_ready")
        vip_ready = sem("vip_ready")
        ip_step = sem("ip_step")
        ip_exp = sem("ip_exp")
        ip_exp_sum = sem("ip_exp_sum")
        ones_ready = sem("ones_ready")
        work_full = sem("work_full")
        work_empty = sem("work_empty")
        out_stored = sem("out_stored")

        def work_number(b, piece, first, last):
            local = work_order(first, last)[piece]
            if first:
                return len(PRO) + local
            return b * LOOP_WORK + (len(PRO) + FIRST_WORK - LOOP_WORK + local)

        def exp_place(n, final):
            return max_bank[:, n % 4, :] if final else exp_bank[:, n % 2, :]

        def batches(eng, body):
            body(0, True, False)
            with eng.Fori(1, B - 1) as b:
                body(b, False, False)
            body(B - 1, False, True)

        block = ctx.enter_context(nc.Block())

        @block.sync
        def _(sp):
            def store_k(b, g):
                sp.wait_ge(k_split, (b * NG + g) * 2 + 2)
                for half in range(2):
                    sp.dma_start(scratch_k[g % NG, :, :, half * HALF:(half + 1) * HALF].rearrange("a r n -> r a n"),
                                 k_parts[half * GR:(half + 1) * GR, :, :]).then_inc(k_stored, 16)

            def store_q(b, g):
                sp.wait_ge(q_step, (b * NG + g) * 4 + 4)
                for half in range(2):
                    sp.dma_start(scratch_q[g % NG, :, :, half * QHALF:(half + 1) * QHALF].rearrange("a r n -> r a n"),
                                 q_parts[half * GR:(half + 1) * GR, :, :]).then_inc(q_stored, 16)

            def q_slot_free(b, g, early_batch):
                if not early_batch:
                    sp.wait_ge(scores_ready, (b * NG + g - NG + 1) * EXPS)

            def slot_free(b, g, early_batch):
                if g == 2:
                    if not early_batch:
                        sp.wait_ge(scores_ready, (b * NG + g - 2) * EXPS)
                elif not early_batch:
                    sp.wait_ge(scores_ready, (b * NG + g - NG + 1) * EXPS)

            def load_k(b, g):
                sp.wait_ge(k_stored, (b * NG + g + 1) * 32)
                for part, (block, count) in reversed(list(enumerate(RUNS))):
                    src = scratch_k[g % NG, part].rearrange("(i h) n -> i (h n)", i=DH)
                    sp.dma_start(k_stack[block * DH:(block + count) * DH, SLOTS[g % NG], :, :].rearrange("p h n -> p (h n)"),
                                 src.unsqueeze(0).to_broadcast([count, DH, GH * KEYS]))\
                      .then_inc(stack_loaded[g % NG], 16)

            def load_q(b, g):
                sp.wait_ge(q_stored, (b * NG + g + 1) * 32)
                for block, count in RUNS:
                    sp.dma_start(q_stack[block * DH:(block + count) * DH, g % NG, :, :].rearrange("p h n -> p (h n)"),
                                 scratch_q[g % NG, 0:count].rearrange("a (i h) n -> (a i) (h n)", i=DH))\
                      .then_inc(stack_loaded[g % NG], 16)

            def stack_group(b, g, early_batch):
                store_k(b, g)
                slot_free(b, g, early_batch)
                load_k(b, g)
                store_q(b, g)
                q_slot_free(b, g, early_batch)
                load_q(b, g)

            def load_ctx(b):
                for c in range(CT):
                    sp.dma_start(ctxt[:, c, :], ctx_t[b, c * 128:(c + 1) * 128, :]).then_inc(ctx_loaded, 16)

            def load_x(b):
                sp.dma_start(xt[:, 0:2, :], x_t[b, 0:256, :].rearrange("(c p) n -> p c n", p=128)).then_inc(x_loaded, 16)
                sp.dma_start(xt[0:64, 2, :], x_t[b, 256:D, :]).then_inc(x_loaded, 16)

            def normalise(group_no):
                sp.wait_ge(o_read, group_no + 1)
                sp.dma_start(sums[:, :], o_sum[DH:128:32, :]).then_inc(sums_loaded, 16)
                sp.wait_ge(recips_ready, group_no + 1)
                sp.dma_start(scratch_r.rearrange("h (c n) -> (h c) n", n=GH * S // 128), recips[:, :])\
                  .then_inc(recips_stored, 16)
                sp.wait_ge(recips_stored, (group_no + 1) * 16)
                sp.dma_start(r_wide[:, :], scratch_r.unsqueeze(1).to_broadcast([GH, 32, S])).then_inc(r_wide_loaded, 16)

            def pack(group_no, g, out_done):
                sp.wait_ge(o_scaled, group_no + 1)
                if out_done is not None:
                    sp.wait_ge(work_full, out_done + 1)
                for h in range(GH):
                    row = (g % 2) * GR + h * DH
                    sp.dma_start(o_t[row:row + DH, g // 2, :], o_sum[h * 32:h * 32 + DH, :]).then_inc(o_packed, 16)

            def store_out(b, t, number):
                sp.wait_ge(work_empty, number + 1)
                sp.dma_start(out[b, t * 128:(t + 1) * 128, :], xres[:, t, :]).then_inc(out_stored, 16)

            sp.dma_start(wk[:, :, :], w_k.rearrange("(c p) n -> p c n", p=128)).then_inc(wk_loaded, 16)
            for c in range(2):
                for ct in range(CT):
                    chunk = lambda a: a.rearrange("p (f c n) -> p f c n", f=2, c=2)[:, :, c, :]
                    sp.dma_start(chunk(ctxt[:, ct, :]), chunk(ctx_t[0, ct * 128:(ct + 1) * 128, :]))\
                      .then_inc(ctx_loaded if c else ctx_first_loaded, 16)
            sp.dma_start(wq[:, 0:2, :], w_q[0:256, :].rearrange("(c p) n -> p c n", p=128)).then_inc(wq_loaded, 16)
            sp.dma_start(wq[0:64, 2, :], w_q[256:D, :]).then_inc(wq_loaded, 16)
            load_x(0)
            sp.dma_start(ctx_ip, ctx_ip_t.rearrange("(c p) n -> p c n", p=128)).then_inc(weights_ip_loaded, 16)
            sp.dma_start(wk_ip, w_k_ip.rearrange("(c p) n -> p c n", p=128)).then_inc(weights_ip_loaded, 16)
            sp.dma_start(wv_ip, w_v_ip.rearrange("(c p) n -> p c n", p=128)).then_inc(weights_ip_loaded, 16)
            sp.dma_start(wv[:, :, :], w_v.rearrange("(c p) n -> p c n", p=128)).then_inc(weights_loaded, 16)
            sp.dma_start(wout[:, 0:2, :], w_out[0:256, :].rearrange("(c p) n -> p c n", p=128)).then_inc(weights_loaded, 16)
            sp.dma_start(wout[0:64, 2, :], w_out[256:D, :]).then_inc(weights_loaded, 16)
            sp.dma_start(wout[96:97, 2, :], b_out.unsqueeze(0)).then_inc(weights_loaded, 16)
            stack_group(0, 0, True)
            stack_group(0, 1, True)

            def body(b, first, last):
                number = lambda piece: work_number(b, piece, first, last)
                for g in range(NG):
                    group_no = b * NG + g
                    if g == 0 and not first:
                        sp.dma_start(xres[:, :, :], x[b - 1].rearrange("(t p) d -> p t d", p=128))\
                          .then_inc(residual_loaded, 16)
                    if g == 3:
                        sp.wait_ge(neg_loaded, (group_no + 1) * 16)
                        load_k(b, 4)
                    if g or not first:
                        normalise(group_no - 1)
                    if g == 1:
                        stack_group(b, 3, first)
                        if not first:
                            for t in range(QT):
                                store_out(b - 1, t, number(("OUT", t)))
                        pack(group_no - 1, 0, None if first else number(("OUT", QT - 1)))
                    elif g or not first:
                        pack(group_no - 1, (g - 1) % NG, None)
                    if g == 0:
                        stack_group(b, 2, first)
                    elif g == 2:
                        if not first:
                            sp.wait_ge(out_stored, b * QT * 16)
                        store_k(b, 4)
                        if not last:
                            sp.wait_ge(work_full, number(("K", 4, 1)) + 1)
                            load_ctx(b + 1)
                        store_q(b, 4)
                        q_slot_free(b, 4, first)
                        load_q(b, 4)
                        if not last:
                            sp.wait_ge(work_full, number(("Q", 4)) + 1)
                            load_x(b + 1)
                    elif g > 2 and not last:
                        stack_group(b, g + 2, False)

            batches(sp, body)
            end = len(PRO) + FIRST_WORK + (B - 2) * LOOP_WORK + len(work_order(False, True))
            sp.dma_start(xres[:, :, :], x[B - 1].rearrange("(t p) d -> p t d", p=128)).then_inc(residual_loaded, 16)
            normalise(B * NG - 1)
            pack(B * NG - 1, NG - 1, None)
            for t in range(QT):
                store_out(B - 1, t, end + t)
            sp.wait_ge(out_stored, B * QT * 16)

        @block.tensor
        def _(pe):
            def k_piece(g, c, ct_range):
                for ct in ct_range:
                    for half in range(2):
                        keys = half * HALF + c * CHUNK
                        last = nc.tensor.matmul(work_bank[half * GR:(half + 1) * GR, 0:CHUNK],
                                                wk[:, ct, (g % NG) * GR:(g % NG + 1) * GR], ctxt[:, ct, keys:keys + CHUNK],
                                                start=(ct == 0), stop=(ct == CT - 1))
                if ct_range[-1] == CT - 1:
                    last.then_inc(work_full, 1)

            def q_piece(g, ct_range):
                for ct in ct_range:
                    rows = (128, 128, 64)[ct]
                    for half in range(2):
                        last = nc.tensor.matmul(work_bank[half * GR:(half + 1) * GR, 0:QHALF],
                                                wq[0:rows, ct, (g % NG) * GR:(g % NG + 1) * GR],
                                                xt[0:rows, ct, half * QHALF:(half + 1) * QHALF],
                                                start=(ct == 0), stop=(ct == 2))
                if ct_range[-1] == 2:
                    last.then_inc(work_full, 1)

            def ip_piece(g, q_number, kip_count):
                pe.wait_ge(work_empty, q_number + 1)
                pe.wait_ge(kip_ready, kip_count)
                for n in range(2):
                    last = nc.tensor.matmul(work_bank[:, n * 64:(n + 1) * 64], q_full[:, n * 128:(n + 1) * 128],
                                            kip_own[:, g % NG, :, :].rearrange("p h t -> p (h t)"), start=True, stop=True)
                last.then_inc(work_full, 1)

            def v_piece(t, ct_range):
                if t < FULL:
                    for ct in ct_range:
                        last = nc.tensor.matmul(work_bank[:, 0:D], ctxt[:, ct, t * 128:(t + 1) * 128], wv[:, ct, :],
                                                start=(ct == 0), stop=(ct == CT - 1))
                else:
                    for ct in ct_range:
                        for odd in range(2):
                            last = nc.tensor.matmul(work_bank[odd * TAIL:odd * TAIL + TAILV, 0:D],
                                                    ctxt[:, ct, FULL * 128:TEXT], wv[:, ct, :],
                                                    start=(ct == 0), stop=(ct == CT - 1))
                if ct_range[-1] == CT - 1:
                    last.then_inc(work_full, 1)

            def out_piece(t, k_range, bank=work_bank[:, 0:D], k_end=3):
                for k in k_range:
                    rows = (128, 128, 97, 128)[k]
                    last = nc.tensor.matmul(bank, o_t[0:rows, k, t * 128:(t + 1) * 128], wout[0:rows, k, :],
                                            start=(k == 0), stop=(k == k_end))
                if k_range[-1] == k_end:
                    last.then_inc(work_full, 1)

            def negative_piece(group_no):
                pe.wait_ge(neg_step, group_no * 5 + 5)
                nc.tensor.transpose(work_bank[:, :].bitcast(BF16)[:, 0:128],
                                    neg_parts[:, :, :].rearrange("p a m -> p (a m)"), ident_b[:, :]).then_inc(work_full, 1)

            def work(b, piece, turn, first, last):
                number = lambda p: work_number(b, p, first, last)
                kind = piece[0]
                if begins(turn):
                    pe.wait_ge(work_empty, number(piece))
                if kind == "K":
                    if piece == ("K", 5, 0):
                        pe.wait_ge(ctx_loaded, (b + 2) * CT * 16)
                    k_piece(piece[1], piece[2], share(CT, turn))
                elif kind == "Q":
                    if piece[1] == 5 and begins(turn):
                        pe.wait_ge(x_loaded, (b + 2) * 32)
                    q_piece(piece[1], share(3, turn))
                elif kind == "IP":
                    ip_piece(piece[1], number(("Q", piece[1])), b + (2 if piece[1] >= NG else 1))
                elif kind == "V":
                    v_piece(piece[1], share(CT, turn))
                elif kind == "OUT":
                    if piece[1] == 0 and begins(turn):
                        pe.wait_ge(o_packed, b * NG * 64)
                    out_piece(piece[1], share(4, turn))
                elif kind == "WA":
                    pe.wait_ge(vip_ready, b + 1)
                    nc.tensor.matmul(work_bank[64:128, 0:D], vip_own[:, 1, :, :].rearrange("p h t -> p (h t)"),
                                     wout[:, 1, :], start=True, stop=True).then_inc(work_full, 1)
                elif kind == "WB":
                    if begins(turn):
                        nc.tensor.matmul(work_bank[0:64, 0:D], vip_own[:, 0, :, :].rearrange("p h t -> p (h t)"),
                                         wout[:, 0, :], start=True, stop=True)
                    if ends(turn):
                        nc.tensor.matmul(work_bank[64:96, 0:D], vip_own[0:64, 2, 0:GH, :].rearrange("p h t -> p (h t)"),
                                         wout[0:64, 2, :], start=True, stop=True).then_inc(work_full, 1)
                elif kind == "TA":
                    pe.wait_ge(ip_step, b * 5 + 5)
                    for t in range(QT):
                        last_mm = nc.tensor.transpose(work_bank[:, t * 128:(t + 1) * 128], p_ip[:, t, 0:128], ident_f[:, :])
                    last_mm.then_inc(work_full, 1)
                elif kind == "TB":
                    for t in range(QT):
                        last_mm = nc.tensor.transpose(work_bank[0:96, t * 128:(t + 1) * 128], p_ip[:, t, 64:160], ident_f[:, :])
                    last_mm.then_inc(work_full, 1)

            def max_unit(group_no, g, u, first_group):
                h, t, half = u // (2 * QT), u // 2 % QT, u % 2
                if not (first_group and u < 2):
                    pe.wait_ge(max_taken, group_no * UNITS + u - 1)
                slot, q_slot = SLOTS[g % NG], g % NG
                for c in range(2):
                    keys = half * HALF + c * CHUNK
                    last = nc.tensor.matmul(max_bank[:, (u % 2) * 2 + c, 0:CHUNK],
                                            q_stack[0:STACK, q_slot, h, t * 128:(t + 1) * 128],
                                            k_stack[0:STACK, slot, h, keys:keys + CHUNK], start=True, stop=True)
                last.then_inc(max_scores, 1)

            def exp_tile(group_no, g, kt, j, first_group, final=False):
                n, slot = kt * GH + j, SLOTS[g]
                bank = exp_place(n, final)
                if final:
                    if n >= 4:
                        pe.wait_ge(probs_ready, group_no * EXPS + n - 3)
                elif not (first_group and n < 2):
                    pe.wait_ge(probs_ready, group_no * EXPS + n - 1)
                if kt < FULL:
                    last = nc.tensor.matmul(bank[:, :], k_stack[0:ROWS, slot, j, kt * 128:(kt + 1) * 128],
                                            q_stack[0:ROWS, g, j, :], start=True, stop=True)
                else:
                    for odd in range(2):
                        h = 2 * j + odd
                        last = nc.tensor.matmul(bank[odd * TAIL:(odd + 1) * TAIL, :],
                                                k_stack[0:ROWS, slot, h, FULL * 128:KEYS], q_stack[0:ROWS, g, h, :],
                                                start=True, stop=True)
                last.then_inc(scores_ready, 1)

            def pv_tile(group_no, g, kt):
                pe.wait_ge(probs_ready, group_no * EXPS + kt * GH + len(exps_of(kt)))
                if kt == 0:
                    pe.wait_ge(o_read, group_no)
                for h in range(GH):
                    head = g * GH + h
                    p = probs[:, kt % 2, h, :] if kt < FULL else probs_tail[:, h // 2, :]
                    last = nc.tensor.matmul(pv_bank[h * 32:h * 32 + VW, :], v_ones[:, kt, head * VW:(head + 1) * VW], p,
                                            start=(kt == 0), stop=(kt == FULL))
                last.then_inc(pv_done, 1)

            def ip_keys():
                for g in range(NG):
                    for half in range(2):
                        for ct in range(CT):
                            last = nc.tensor.matmul(work_bank[half * GR:(half + 1) * GR, g * 64:(g + 1) * 64],
                                                    wk_ip[:, ct, g * GR:(g + 1) * GR], ctx_ip[:, ct, :],
                                                    start=(ct == 0), stop=(ct == CT - 1))
                last.then_inc(work_full, 1)

            def ip_values():
                for m, rows in enumerate((128, 128, 64)):
                    for ct in range(CT):
                        last = nc.tensor.matmul(work_bank[0:rows, m * 64:(m + 1) * 64],
                                                wv_ip[:, ct, m * 128:m * 128 + rows], ctx_ip[:, ct, :],
                                                start=(ct == 0), stop=(ct == CT - 1))
                last.then_inc(work_full, 1)

            units = iter(range(UNITS))
            pe.wait_ge(wk_loaded, 16)
            pe.wait_ge(ctx_first_loaded, CT * 16)
            for piece, turn, beside in PRO_PLAN:
                number = PRO_ORDER[piece]
                if number and begins(turn):
                    pe.wait_ge(work_empty, number)
                if piece[0] == "K":
                    if piece == ("K", 0, 1):
                        pe.wait_ge(ctx_loaded, CT * 16)
                    k_piece(piece[1], piece[2], share(CT, turn))
                elif piece[0] == "Q":
                    pe.wait_ge(wq_loaded, 32)
                    pe.wait_ge(x_loaded, 32)
                    q_piece(piece[1], share(3, turn))
                elif piece[0] == "KIP":
                    pe.wait_ge(weights_ip_loaded, 48)
                    ip_keys()
                elif piece[0] == "IP":
                    ip_piece(piece[1], PRO_ORDER["Q", piece[1]], 1)
                elif piece[0] == "VIP":
                    ip_values()
                elif piece[0] == "V":
                    pe.wait_ge(weights_loaded, 64)
                    v_piece(piece[1], share(CT, turn))
                else:
                    pe.wait_ge(cleared, 8)
                    negative_piece(0)
                for _ in range(beside):
                    u = next(units)
                    if u == 0:
                        pe.wait_ge(stack_loaded[0], 96)
                    max_unit(0, 0, u, True)
            pe.wait_ge(consts_loaded, 80)
            pe.wait_ge(ones_ready, 1)

            def body(b, first, last):
                plan = work_plan(first, last)
                for g in range(NG):
                    group_no = b * NG + g
                    units = iter(range(UNITS))

                    def next_units(n):
                        for _ in range(n):
                            u = next(units)
                            if u == 0:
                                nb = b + 1 if g < NG - 1 else b + 2
                                pe.wait_ge(stack_loaded[(g + 1) % NG], nb * 96)
                            max_unit(group_no + 1, g + 1, u, False)

                    pe.wait_ge(neg_loaded, (group_no + 1) * 16)
                    if last and g == NG - 1:
                        for kt in range(KT):
                            for j in exps_of(kt)[:3]:
                                exp_tile(group_no, g, kt, j, False, True)
                            pv_tile(group_no if kt else group_no - 1, g if kt else g - 1, (kt - 1) % KT)
                            if kt < FULL:
                                exp_tile(group_no, g, kt, 3, False, True)
                        continue
                    for kt in range(KT):
                        places = units_at(g, kt)
                        exp_tile(group_no, g, kt, 0, first and g == 0)
                        next_units(places[0])
                        exp_tile(group_no, g, kt, 1, first and g == 0)
                        if kt == NEG_AT and not (last and g == NG - 1):
                            pe.wait_ge(work_empty, work_number(b, ("NEG", g + 1), first, last))
                            negative_piece(group_no + 1)
                        made_late = kt - 1 if g == 0 else FULL if (g, kt) == (1, 0) else 0
                        if made_late >= V_EARLY:
                            pe.wait_ge(work_empty, work_number(b, ("V", made_late), first, last) + 1)
                        if kt:
                            pv_tile(group_no, g, kt - 1)
                        elif g or not first:
                            pv_tile(group_no - 1, (g - 1) % NG, FULL)
                        next_units(places[1])
                        if kt < FULL:
                            exp_tile(group_no, g, kt, 2, first and g == 0)
                            next_units(places[2])
                            exp_tile(group_no, g, kt, 3, first and g == 0)
                        if (g, kt) in plan:
                            work(b, *plan[g, kt], first, last)
                        next_units(places[3])

            batches(pe, body)
            pv_tile(B * NG - 1, NG - 1, FULL)
            pe.wait_ge(o_packed, (B * NG - 1) * 64)
            for t in range(QT):
                out_piece(t, (0, 1, 3), max_bank[:, t, 0:D], 2)
            pe.wait_ge(o_packed, B * NG * 64)
            for t in range(QT):
                out_piece(t, (2,), max_bank[:, t, 0:D], 2)

        @block.scalar
        def _(act):
            def copy(dst, src):
                return nc.scalar.activation(dst, src, ACT.Copy)

            def k_first_part(b, g, c, number):
                act.wait_ge(work_full, number + 1)
                if c == 0:
                    act.wait_ge(k_stored, (b * NG + g) * 32)
                copy(k_parts[:, 0, c * CHUNK:(c + 1) * CHUNK], work_bank[:, 0:CHUNK]).then_inc(k_high, 1)

            def q_copy(b, g, number):
                act.wait_ge(work_full, number + 1)
                act.wait_ge(q_step, (b * NG + g) * 4)
                copy(q_full[:, :], work_bank[:, 0:QHALF]).then_inc(work_empty, 1)

            def v_copy(b, t, number, reused):
                act.wait_ge(work_full, number + 1)
                if reused:
                    act.wait_ge(pv_done, (b * NG - 1) * KT + t + 1)
                v = v_ones[:, t, :].rearrange("p (h d) -> p h d", d=VW)
                w = work_bank[:, 0:D].rearrange("p (h d) -> p h d", d=DH)
                if t < FULL:
                    copy(v[:, :, 0:DH], w[:, :, :]).then_inc(work_empty, 1)
                else:
                    copy(v[0:TAILV, 0:HEADS:2, 0:DH], w[0:TAILV, 0:HEADS:2, :])
                    copy(v[TAIL:TAIL + TAILV, 1:HEADS:2, 0:DH], w[TAIL:TAIL + TAILV, 1:HEADS:2, :]).then_inc(work_empty, 1)

            def negative_copy(group_no, g, number, first_group):
                act.wait_ge(work_full, number + 1)
                if not first_group:
                    act.wait_ge(neg_loaded, group_no * 16)
                copy(neg_rows[:, :], work_bank[:, :].bitcast(BF16)[0:PARTS * UNITS // 2, 0:128]).then_inc(work_empty, 1)
                act.wait_ge(work_empty, number + 1)
                act.dma_start(q_stack[STACK:ROWS, g % NG, :, :], neg_rows[:, :]).then_inc(neg_loaded, 16)

            def exp_tile(group_no, kt, j, first_group, final):
                n = kt * GH + j
                act.wait_ge(scores_ready, group_no * EXPS + n + 1)
                if j == 0:
                    if kt == FULL:
                        if not first_group:
                            act.wait_ge(pv_done, group_no * KT)
                    elif kt >= 2:
                        act.wait_ge(pv_done, group_no * KT + kt - 1)
                    elif not first_group:
                        act.wait_ge(pv_done, group_no * KT + kt - 2)
                dst = probs[:, kt % 2, j, :] if kt < FULL else probs_tail[:, j, :]
                nc.scalar.activation(dst, exp_place(n, final), ACT.Exp, scale=SCALE).then_inc(probs_ready, 1)

            def o_copy(group_no):
                act.wait_ge(pv_done, (group_no + 1) * KT)
                act.wait_ge(o_packed, group_no * 64)
                copy(o_sum[:, :], pv_bank[:, :]).then_inc(o_read, 1)

            for piece in PRO:
                number = PRO_ORDER[piece]
                if piece[0] == "K":
                    k_first_part(0, piece[1], piece[2], number)
                elif piece[0] == "Q":
                    q_copy(0, piece[1], number)
                elif piece[0] == "KIP":
                    act.wait_ge(work_full, number + 1)
                    copy(kip[:, :, :].rearrange("p g n -> p (g n)"), work_bank[:, 0:D]).then_inc(work_empty, 1)
                elif piece[0] == "VIP":
                    act.wait_ge(work_full, number + 1)
                    copy(vip[:, 0:2, :].rearrange("p m n -> p (m n)"), work_bank[:, 0:128])
                    copy(vip[0:64, 2, :], work_bank[0:64, 128:192]).then_inc(work_empty, 1)
                    act.wait_ge(cleared, 8)
                elif piece[0] == "V":
                    v_copy(0, piece[1], number, False)
                elif piece[0] == "NEG":
                    negative_copy(0, 0, number, True)

            def body(b, first, last):
                plan = work_plan(first, last)
                for g in range(NG):
                    group_no = b * NG + g
                    for kt in range(KT):
                        tiles = list(exps_of(kt))
                        for j in tiles[:2]:
                            exp_tile(group_no, kt, j, first and g == 0, last and g == NG - 1)
                        if kt == 0 and (g or not first):
                            o_copy(group_no - 1)
                        if kt == NEG_AT and not (last and g == NG - 1):
                            negative_copy(group_no + 1, g + 1, work_number(b, ("NEG", g + 1), first, last), False)
                        for j in tiles[2:]:
                            exp_tile(group_no, kt, j, first and g == 0, last and g == NG - 1)
                        if (g, kt) == (3, 0):
                            act.wait_ge(ip_step, b * 5 + 3)
                            nc.scalar.activation(s_ip[:, :, :], s_ip[:, :, :], ACT.Exp).then_inc(ip_exp, 1)
                        piece, turn = plan.get((g, kt), (None, None))
                        if not ends(turn):
                            continue
                        kind, number = piece[0], work_number(b, piece, first, last)
                        if kind == "K":
                            k_first_part(b, piece[1], piece[2], number)
                        elif kind == "Q":
                            q_copy(b, piece[1], number)
                        elif kind == "V":
                            if piece[1] >= V_EARLY:
                                v_copy(b, piece[1], number, not first)
                            else:
                                v_copy(b + 1, piece[1], number, True)
                        elif kind == "WA":
                            act.wait_ge(work_full, number + 1)
                            copy(wout[64:128, 3, :], work_bank[64:128, 0:D]).then_inc(work_empty, 1)
                        elif kind == "WB":
                            act.wait_ge(work_full, number + 1)
                            copy(wout[0:64, 3, :], work_bank[0:64, 0:D])
                            copy(wout[64:96, 2, :], work_bank[64:96, 0:D]).then_inc(work_empty, 1)
                        elif kind == "TA":
                            act.wait_ge(work_full, number + 1)
                            copy(o_t[:, 3, :], work_bank[:, :]).then_inc(work_empty, 1)
                        elif kind == "TB":
                            act.wait_ge(work_full, number + 1)
                            copy(o_t[64:96, 2, :], work_bank[64:96, :]).then_inc(work_empty, 1)

            batches(act, body)
            o_copy(B * NG - 1)

        @block.vector
        def _(dve):
            def k_remainder(b, g, c, number, reused=True):
                dve.wait_ge(k_high, (b * NG + g) * 2 + c + 1)
                if reused:
                    dve.wait_ge(k_split, (b * NG + g) * 2 + c - 1)
                nc.vector.tensor_tensor(k_rest[:, c, :], work_bank[:, 0:CHUNK], k_parts[:, 0, c * CHUNK:(c + 1) * CHUNK],
                                        ALU.subtract).then_inc(work_empty, 1)

            def ip_scale(g, number):
                dve.wait_ge(work_full, number + 1)
                src = work_bank[:, 0:128].rearrange("p (n f m) -> p n f m", n=2, f=2)
                for half in range(2):
                    last = nc.vector.tensor_scalar(
                        s_ip[:, half * 2:half * 2 + 2, (g % NG) * 32:(g % NG + 1) * 32], src[:, :, half, :], SCALE, None, ALU.mult)
                last.then_inc(work_empty, 1)

            def take_max(group_no, u):
                dve.wait_ge(max_scores, group_no * UNITS + u + 1)
                nc.vector.reduce_max(half_max[:, u:u + 1], max_bank[:, (u % 2) * 2:(u % 2) * 2 + 2, 0:CHUNK], AX.XY)\
                  .then_inc(max_taken, 1)

            def negative_parts(group_no):
                dve.wait_ge(max_taken, (group_no + 1) * UNITS)
                nc.vector.reduce_max(neg_max[:, :], half_max[:, :].rearrange("p (m f) -> p m f", f=2), AX.X, negate=True)\
                  .then_inc(neg_step, 1)
                dve.wait_ge(neg_step, group_no * 5 + 1)
                nc.vector.tensor_copy(neg_parts[:, 0, :], neg_max[:, :]).then_inc(neg_step, 1)
                dve.wait_ge(neg_step, group_no * 5 + 2)
                nc.vector.tensor_tensor(neg_rest[:, :], neg_max[:, :], neg_parts[:, 0, :], ALU.subtract).then_inc(neg_step, 1)
                dve.wait_ge(neg_step, group_no * 5 + 3)
                nc.vector.tensor_copy(neg_parts[:, 1, :], neg_rest[:, :]).then_inc(neg_step, 1)
                dve.wait_ge(neg_step, group_no * 5 + 4)
                nc.vector.tensor_tensor(neg_parts[:, 2, :], neg_rest[:, :], neg_parts[:, 1, :], ALU.subtract)\
                  .then_inc(neg_step, 1)

            def invert_sums(group_no):
                dve.wait_ge(sums_loaded, (group_no + 1) * 16)
                dve.wait_ge(recips_stored, group_no * 16)
                nc.vector.reciprocal(recips[:, :], sums[:, :]).then_inc(recips_ready, 1)

            def ip_softmax_1(b, number):
                scores = s_ip[:, :, :].rearrange("p q (h t) -> p q h t", t=IPT)
                m = mask[:, bass.ds(b, 1), :, :].rearrange("p o q t -> p (o q) t")
                dve.wait_ge(work_empty, number + 1)
                nc.vector.tensor_tensor(scores, scores, m.unsqueeze(2).to_broadcast([128, QT, HEADS, IPT]), ALU.add)\
                  .then_inc(ip_step, 1)
                dve.wait_ge(ip_step, b * 5 + 1)
                nc.vector.reduce_max(ip_max[:, :, :], scores, AX.X).then_inc(ip_step, 1)
                dve.wait_ge(ip_step, b * 5 + 2)
                nc.vector.tensor_tensor(scores, scores, ip_max[:, :, :].unsqueeze(3).to_broadcast([128, QT, HEADS, IPT]),
                                        ALU.subtract).then_inc(ip_step, 1)

            def ip_softmax_2(b):
                scores = s_ip[:, :, :].rearrange("p q (h t) -> p q h t", t=IPT)
                dve.wait_ge(ip_exp, b + 1)
                nc.vector.reduce_sum(ip_sum[:, :, :], scores, AX.X).then_inc(ip_exp_sum, 1)
                dve.wait_ge(ip_exp_sum, b + 1)
                nc.vector.reciprocal(ip_max[:, :, :], ip_sum[:, :, :]).then_inc(ip_step, 1)
                dve.wait_ge(ip_step, b * 5 + 4)
                nc.vector.tensor_tensor(p_ip[:, :, :].rearrange("p q (h t) -> p q h t", t=IPT), scores,
                                        ip_max[:, :, :].unsqueeze(3).to_broadcast([128, QT, HEADS, IPT]), ALU.mult)\
                  .then_inc(ip_step, 1)

            def out_add(b, t, number, src):
                dve.wait_ge(work_full, number + 1)
                if t == 0:
                    dve.wait_ge(residual_loaded, b * 16)
                nc.vector.tensor_tensor(xres[:, t, :], src, xres[:, t, :], ALU.add)\
                  .then_inc(work_empty, 1)

            nc.vector.memset(pv_bank[:, :], 0.0).then_inc(cleared, 1)
            nc.vector.memset(v_ones[:, :, :], 0.0).then_inc(mask_step, 1)
            dve.wait_ge(mask_step, 1)
            v = v_ones[:, :, :].rearrange("p t (h d) -> p t h d", d=VW)
            nc.vector.memset(v[:, 0:FULL, :, DH], 1.0).then_inc(cleared, 1)
            nc.vector.memset(v[0:TAILV, FULL, 0:HEADS:2, DH], 1.0).then_inc(cleared, 1)
            nc.vector.memset(v[TAIL:TAIL + TAILV, FULL, 1:HEADS:2, DH], 1.0).then_inc(cleared, 1)
            nc.vector.memset(o_t[96:97, 2, :], 1.0).then_inc(cleared, 1)

            dve.wait_ge(consts_loaded, 80)
            nc.vector.tensor_copy(ident_b[:, :], ident_f[:, :]).then_inc(cleared, 1)

            nc.vector.memset(neg_parts[:, :, :], 0.0).then_inc(cleared, 1)
            nc.vector.memset(zero[:, :], 0.0).then_inc(cleared, 1)

            tests = ((0, 0, ALU.is_ge), (1, 1, ALU.is_ge), (0, 2, ALU.is_le), (1, 3, ALU.is_le))
            step = 1
            for n, (axis, corner, op) in enumerate(tests):
                place = grid_sb[:, axis, :].unsqueeze(1).unsqueeze(3).to_broadcast([128, B, QT, 4])
                limit = box[:, :, :, corner].unsqueeze(2).to_broadcast([128, B, QT, 4])
                nc.vector.tensor_tensor((cmp if n else inside)[:, :, :, :], place, limit, op).then_inc(mask_step, 1)
                step += 1
                dve.wait_ge(mask_step, step)
                if n:
                    nc.vector.tensor_tensor(inside[:, :, :, :], inside[:, :, :, :], cmp[:, :, :, :], ALU.mult)\
                      .then_inc(mask_step, 1)
                    step += 1
                    dve.wait_ge(mask_step, step)
            nc.vector.tensor_scalar(mask[:, :, :, IPT // 2:IPT], inside[:, :, :, :], -NEG, NEG, ALU.mult, ALU.add)\
              .then_inc(mask_step, 1)
            nc.vector.reduce_max(outside[:, :, :], inside[:, :, :, :], AX.X).then_inc(mask_step, 1)
            dve.wait_ge(mask_step, step + 2)
            nc.vector.tensor_scalar(mask[:, :, :, 0:IPT // 2], outside[:, :, :].unsqueeze(3).to_broadcast([128, B, QT, 4]),
                                    NEG, None, ALU.mult).then_inc(mask_step, 1)
            dve.wait_ge(mask_step, step + 3)

            units = iter(range(UNITS))
            for piece, turn, beside in PRO_PLAN:
                if piece[0] == "K" and ends(turn):
                    k_remainder(0, piece[1], piece[2], PRO_ORDER[piece], piece[1] > 0)
                elif piece[0] == "IP":
                    ip_scale(piece[1], PRO_ORDER[piece])
                for _ in range(beside):
                    take_max(0, next(units))
            negative_parts(0)

            def body(b, first, last):
                plan = work_plan(first, last)
                for g in range(NG):
                    group_no = b * NG + g
                    units = iter(range(UNITS))
                    for kt in range(KT):
                        places = (0,) * 4 if last and g == NG - 1 else units_at(g, kt)
                        for _ in range(sum(places)):
                            u = next(units)
                            take_max(group_no + 1, u)
                            if u == UNITS - 1:
                                negative_parts(group_no + 1)
                        if (g, kt) == (2, FULL):
                            ip_softmax_1(b, work_number(b, ("IP", 4), first, last))
                        piece, turn = plan.get((g, kt), (None, None))
                        if kt == INVERT_AT[g] and (g or not first):
                            invert_sums(group_no - 1)
                        if ends(turn):
                            number = work_number(b, piece, first, last)
                            if piece[0] == "K":
                                k_remainder(b, piece[1], piece[2], number)
                            elif piece[0] == "IP":
                                ip_scale(piece[1], number)
                            elif piece[0] == "OUT":
                                out_add(b, piece[1], number, work_bank[:, 0:D])
                        if (g, kt) == (3, 1):
                            ip_softmax_2(b)

            batches(dve, body)
            end = len(PRO) + FIRST_WORK + (B - 2) * LOOP_WORK + len(work_order(False, True))
            invert_sums(B * NG - 1)
            for t in range(QT):
                out_add(B, t, end + t, max_bank[:, t, 0:D])

        @block.gpsimd
        def _(pool):
            def split_k(b, g, c, number):
                pool.wait_ge(work_empty, number + 1)
                part = k_parts[:, :, c * CHUNK:(c + 1) * CHUNK]
                nc.gpsimd.tensor_tensor(part[:, 1, :], k_rest[:, c, :], zero[:, :].to_broadcast([128, CHUNK]), ALU.add)\
                  .then_inc(k_mid, 1)
                pool.wait_ge(k_mid, (b * NG + g) * 2 + c + 1)
                nc.gpsimd.tensor_tensor(part[:, 2, :], k_rest[:, c, :], part[:, 1, :], ALU.subtract).then_inc(k_split, 1)

            def split_q(b, g, number):
                done = (b * NG + g) * 4
                pool.wait_ge(work_empty, number + 1)
                pool.wait_ge(q_stored, (b * NG + g) * 32)
                nc.gpsimd.tensor_tensor(q_parts[:, 0, :], q_full[:, :], zero[:, :].to_broadcast([128, QHALF]), ALU.add)\
                  .then_inc(q_step, 1)
                pool.wait_ge(q_step, done + 1)
                nc.gpsimd.tensor_tensor(q_rest[:, :], q_full[:, :], q_parts[:, 0, :], ALU.subtract).then_inc(q_step, 1)
                pool.wait_ge(q_step, done + 2)
                nc.gpsimd.tensor_tensor(q_parts[:, 1, :], q_rest[:, :], zero[:, :].to_broadcast([128, QHALF]), ALU.add)\
                  .then_inc(q_step, 1)
                pool.wait_ge(q_step, done + 3)
                nc.gpsimd.tensor_tensor(q_parts[:, 2, :], q_rest[:, :], q_parts[:, 1, :], ALU.subtract).then_inc(q_step, 1)

            def own_k(b):
                src = kip[:, :, bass.ds(b * IPT, IPT)].unsqueeze(2).to_broadcast([128, NG, 8, IPT])
                nc.gpsimd.tensor_tensor(kip_own[:, :, :, :], src,
                                        own_k_sb[:, :].unsqueeze(1).unsqueeze(3).to_broadcast([128, NG, 8, IPT]), ALU.mult)\
                  .then_inc(kip_ready, 1)

            def own_v(b):
                src = vip[:, :, bass.ds(b * IPT, IPT)]
                nc.gpsimd.tensor_tensor(vip_own[:, 0:2, :, :], src[:, 0:2, :].unsqueeze(2).to_broadcast([128, 2, 8, IPT]),
                                        own_v_sb[:, :].unsqueeze(1).unsqueeze(3).to_broadcast([128, 2, 8, IPT]), ALU.mult)
                nc.gpsimd.tensor_tensor(vip_own[0:64, 2, 0:GH, :], src[0:64, 2, :].unsqueeze(1).to_broadcast([64, GH, IPT]),
                                        own_v_sb[0:64, 0:GH].unsqueeze(2).to_broadcast([64, GH, IPT]), ALU.mult).then_inc(vip_ready, 1)

            def scale_o(group_no):
                pool.wait_ge(r_wide_loaded, (group_no + 1) * 16)
                nc.gpsimd.tensor_tensor(o_sum[:, :], o_sum[:, :], r_wide[:, :], ALU.mult).then_inc(o_scaled, 1)

            pool.dma_start(own_k_sb[:, :], own_k_rows).then_inc(consts_loaded, 16)
            pool.dma_start(own_v_sb[:, :], own_v_rows).then_inc(consts_loaded, 16)
            pool.dma_start(ident_f[:, :], ident).then_inc(consts_loaded, 16)
            pool.dma_start(grid_sb[:, :, :], grid).then_inc(consts_loaded, 16)
            pool.dma_start(box[:, :, :, :].rearrange("p b m k -> p (b m k)"),
                           boxes.rearrange("b m k -> (b m k)").partition_broadcast(128)).then_inc(consts_loaded, 16)
            pool.wait_ge(consts_loaded, 80)
            pool.wait_ge(cleared, 8)
            for g in range(2):
                if g == 1:
                    pool.wait_ge(work_empty, PRO_ORDER["KIP",] + 1)
                    own_k(0)
                for c in range(2):
                    split_k(0, g, c, PRO_ORDER["K", g, c])
                split_q(0, g, PRO_ORDER["Q", g])
            pool.wait_ge(q_step, 8)
            nc.gpsimd.memset(k_stack[STACK:ROWS, :, :, :], 1.0).then_inc(ones_ready, 1)
            pool.wait_ge(ones_ready, 1)

            def body(b, first, last):
                number = lambda piece: work_number(b, piece, first, last)
                for g in range(NG):
                    splits = [p for p in SPLITS[g] if not (last and p[1] > 4)]
                    for n, piece in enumerate(splits):
                        if n == SCALE_AT[g] and (g or not first):
                            scale_o(b * NG + g - 1)
                        if piece[0] == "K":
                            split_k(b, piece[1], piece[2], number(piece))
                        else:
                            split_q(b, piece[1], number(piece))
                    if len(splits) <= SCALE_AT[g]:
                        scale_o(b * NG + g - 1)
                    if g == 1:
                        own_v(b)
                    if g == 2 and not last:
                        pool.wait_ge(work_full, number(("IP", 4)) + 1)
                        own_k(b + 1)

            batches(pool, body)
            scale_o(B * NG - 1)


def kernel(x, ctx_2048, fside_Bx4x4_0, L0_xattn_w_q, L0_xattn_w_k, L0_xattn_w_v, L0_xattn_w_k_ip, L0_xattn_w_v_ip,
           L0_xattn_w_out, L0_xattn_b_out):
    import concourse.bacc as bacc
    from concourse.bass_utils import run_bass_kernel_spmd

    x, ctx = np.asarray(x), np.asarray(ctx_2048)
    text = np.concatenate([ctx[:, :TEXT], ctx[:, :KEYS - TEXT]], axis=1)
    q = np.arange(S)
    step_x = (np.arange(GRID_W, dtype=np.float32) / np.float32(GRID_W - 1)).astype(np.float32)
    step_y = (np.arange(GRID_H, dtype=np.float32) / np.float32(GRID_H - 1)).astype(np.float32)
    places = np.stack([step_x[q % GRID_W], step_y[q // GRID_W]])
    rows = np.arange(128)[:, None]

    def dims_first(w):
        w = np.asarray(w)
        return w.reshape(-1, NG, GH, DH).transpose(0, 1, 3, 2).reshape(w.shape)

    arrays = {
        "x": x,
        "x_t": x.transpose(0, 2, 1),
        "ctx_t": text.transpose(0, 2, 1),
        "ctx_ip_t": ctx[:, TEXT:].transpose(2, 0, 1).reshape(C, B * IPT),
        "boxes": np.asarray(fside_Bx4x4_0),
        "grid": places.reshape(2, QT, 128).transpose(2, 0, 1),
        "own_k_rows": (rows // GR * GH + rows % GH == np.arange(8)[None, :]).astype(np.float32),
        "own_v_rows": (rows // DH == np.arange(8)[None, :]).astype(np.float32),
        "ident": np.eye(128, dtype=np.float32),
        "w_q": dims_first(L0_xattn_w_q), "w_k": dims_first(L0_xattn_w_k), "w_v": L0_xattn_w_v,
        "w_k_ip": dims_first(L0_xattn_w_k_ip),
        "w_v_ip": L0_xattn_w_v_ip, "w_out": L0_xattn_w_out, "b_out": L0_xattn_b_out,
    }
    nc = bacc.Bacc("TRN2", target_bir_lowering=False, num_devices=1)
    feeds, args = {}, []
    for name, a in arrays.items():
        a = np.ascontiguousarray(a)
        feeds[f"in_{name}"] = a
        args.append(nc.dram_tensor(f"in_{name}", a.shape, mybir.dt.from_np(a.dtype), kind="ExternalInput").ap())
    out = nc.dram_tensor("out", (B, S, D), FP32, kind="ExternalOutput").ap()
    cross_attention(nc, *args, out)
    r = run_bass_kernel_spmd(nc, [feeds], core_ids=[0])
    return r.results[0]["out"]
```
